# Optimizing a Trainium2 kernel written in Bass

```python
import numpy as np
import jax
import jax.numpy as jnp

def _softmax(x, axis=-1):
    return jax.nn.softmax(x, axis=axis)

def _gelu(x):
    return jax.nn.gelu(x, approximate=True)

def _silu(x):
    return jax.nn.silu(x)

def _sigmoid(x):
    return jax.nn.sigmoid(x)

def _layernorm(x, axis=-1, eps=1e-05):
    m = jnp.mean(x, axis=axis, keepdims=True)
    v = jnp.var(x, axis=axis, keepdims=True)
    return (x - m) / jnp.sqrt(v + eps)

def _scatter_add(tgt, idx, src, axis=0):
    return tgt.at[idx].add(src)

def _segment_sum(src, seg, n):
    return jax.ops.segment_sum(src, seg, n)
kernel_name = 'mk_prb_d1_jaxref_r8_eec916'

def setup_inputs(seed: int=0):
    np.random.seed(seed)
    _w = jnp.asarray

    def _L0_attn_setup():
        import jax, jax.numpy as jnp
        import numpy as np
        B, T, HID = (2, 256, 256)
        H, DK, DV = (16, 128, 128)
        KC = 4
        EPS = 1e-06

        def short_conv(x, w):
            Tn = x.shape[1]
            xp = jnp.pad(x, ((0, 0), (KC - 1, 0), (0, 0)))
            out = xp[:, 0:Tn, :] * w[:, 0]
            for i in range(1, KC):
                out = out + xp[:, i:i + Tn, :] * w[:, i]
            return jax.nn.silu(out)

        def _l2norm(x):
            x = x.astype(jnp.float32)
            return x * jax.lax.rsqrt(jnp.sum(x * x, -1, keepdims=True) + 1e-06)
        key = jax.random.key(seed)
        ks = jax.random.split(key, 16)
        s = 0.02
        mk = lambda k, shp, sc=s: jax.random.normal(k, shp, jnp.float32) * sc
        a_init = jax.random.uniform(ks[7], (H,), minval=1.0, maxval=16.0, dtype=jnp.float32)
        return {'hidden_states': jax.random.normal(ks[0], (B, T, HID), jnp.float32), 'Wq': mk(ks[1], (HID, H * DK)), 'Wk': mk(ks[2], (HID, H * DK)), 'Wv': mk(ks[3], (HID, H * DV)), 'conv_q': mk(ks[4], (H * DK, KC), 0.3), 'conv_k': mk(ks[5], (H * DK, KC), 0.3), 'conv_v': mk(ks[6], (H * DV, KC), 0.3), 'A_log': jnp.log(a_init).reshape(1, 1, H, 1), 'Wfa': mk(ks[8], (HID, DV)), 'Wfb': mk(ks[9], (DV, H * DV)), 'dt_bias': jnp.zeros((H * DV,), jnp.float32), 'Wb': mk(ks[10], (HID, H)), 'Wga': mk(ks[11], (HID, DV)), 'Wgb': mk(ks[12], (DV, H * DV)), 'norm_w': jnp.ones((DV,), jnp.float32), 'Wo': mk(ks[13], (H * DV, HID))}
    _L0_attn_in = _L0_attn_setup()

    def _L0_ffn_setup():
        import jax, jax.numpy as jnp
        import numpy as np
        D_MODEL = 256
        D_EXPERT = 1024
        EPS = 1e-08

        def ternary_quant(w):
            scale = jnp.mean(jnp.abs(w)) + EPS
            q = jnp.clip(jnp.round(w / scale), -1.0, 1.0) * scale
            return w + jax.lax.stop_gradient(q - w)
        key = jax.random.key(seed)
        k_x, k_up, k_gate, k_down = jax.random.split(key, 4)
        std_in = 1.0 / np.sqrt(D_MODEL)
        std_exp = 1.0 / np.sqrt(D_EXPERT)
        return {'x': jax.random.normal(k_x, (4, 256, D_MODEL), dtype=jnp.float32), 'W_up': jax.random.normal(k_up, (D_EXPERT, D_MODEL), dtype=jnp.float32) * std_in, 'W_gate': jax.random.normal(k_gate, (D_EXPERT, D_MODEL), dtype=jnp.float32) * std_in, 'W_down': jax.random.normal(k_down, (D_MODEL, D_EXPERT), dtype=jnp.float32) * std_exp}
    _L0_ffn_in = _L0_ffn_setup()
    _d = {'L0_attn_hidden_states': _L0_attn_in['hidden_states'], 'L0_attn_Wq': _L0_attn_in['Wq'], 'L0_attn_Wk': _L0_attn_in['Wk'], 'L0_attn_Wv': _L0_attn_in['Wv'], 'L0_attn_conv_q': _L0_attn_in['conv_q'], 'L0_attn_conv_k': _L0_attn_in['conv_k'], 'L0_attn_conv_v': _L0_attn_in['conv_v'], 'L0_attn_A_log': _L0_attn_in['A_log'], 'L0_attn_Wfa': _L0_attn_in['Wfa'], 'L0_attn_Wfb': _L0_attn_in['Wfb'], 'L0_attn_dt_bias': _L0_attn_in['dt_bias'], 'L0_attn_Wb': _L0_attn_in['Wb'], 'L0_attn_Wga': _L0_attn_in['Wga'], 'L0_attn_Wgb': _L0_attn_in['Wgb'], 'L0_attn_norm_w': _L0_attn_in['norm_w'], 'L0_attn_Wo': _L0_attn_in['Wo'], 'L0_ffn_W_up': _L0_ffn_in['W_up'], 'L0_ffn_W_gate': _L0_ffn_in['W_gate'], 'L0_ffn_W_down': _L0_ffn_in['W_down']}
    _x0 = _d['L0_attn_hidden_states']
    _d['L0_attn_hidden_states'] = jax.random.normal(jax.random.fold_in(jax.random.key(seed), 1), (16, 256, 256), dtype=_x0.dtype)
    del _x0
    return _d

def reference(L0_attn_hidden_states, L0_attn_Wq, L0_attn_Wk, L0_attn_Wv, L0_attn_conv_q, L0_attn_conv_k, L0_attn_conv_v, L0_attn_A_log, L0_attn_Wfa, L0_attn_Wfb, L0_attn_dt_bias, L0_attn_Wb, L0_attn_Wga, L0_attn_Wgb, L0_attn_norm_w, L0_attn_Wo, L0_ffn_W_up, L0_ffn_W_gate, L0_ffn_W_down):

    def _L0_attn_ref(hidden_states, Wq, Wk, Wv, conv_q, conv_k, conv_v, A_log, Wfa, Wfb, dt_bias, Wb, Wga, Wgb, norm_w, Wo):
        import jax, jax.numpy as jnp
        import numpy as np
        B, T, HID = (2, 256, 256)
        H, DK, DV = (16, 128, 128)
        KC = 4
        EPS = 1e-06

        def short_conv(x, w):
            Tn = x.shape[1]
            xp = jnp.pad(x, ((0, 0), (KC - 1, 0), (0, 0)))
            out = xp[:, 0:Tn, :] * w[:, 0]
            for i in range(1, KC):
                out = out + xp[:, i:i + Tn, :] * w[:, i]
            return jax.nn.silu(out)

        def _l2norm(x):
            x = x.astype(jnp.float32)
            return x * jax.lax.rsqrt(jnp.sum(x * x, -1, keepdims=True) + 1e-06)
        Bn, Tn, _ = hidden_states.shape
        q = short_conv(hidden_states @ Wq, conv_q).reshape(Bn, Tn, H, DK)
        k = short_conv(hidden_states @ Wk, conv_k).reshape(Bn, Tn, H, DK)
        v = short_conv(hidden_states @ Wv, conv_v).reshape(Bn, Tn, H, DV)
        g = (hidden_states @ Wfa @ Wfb).astype(jnp.float32)
        g = g.reshape(Bn, Tn, H, DV) + dt_bias.astype(jnp.float32).reshape(1, 1, H, DV)
        g = jnp.exp(-jax.nn.softplus(g) * jnp.exp(A_log.astype(jnp.float32)))
        beta = jax.nn.sigmoid((hidden_states @ Wb).astype(jnp.float32))
        q = _l2norm(q) * DK ** (-0.5)
        k = _l2norm(k)
        vf = v.astype(jnp.float32)

        def step(S, inp):
            qt, kt, vt, gt, bt = inp
            S = S * gt[..., None]
            pred = jnp.einsum('bhk,bhkv->bhv', kt, S)
            delta = (vt - pred) * bt[..., None]
            S = S + kt[..., None] * delta[:, :, None, :]
            o = jnp.einsum('bhk,bhkv->bhv', qt, S)
            return (S, o)
        tfirst = lambda x: jnp.moveaxis(x, 1, 0)
        S0 = jnp.zeros((Bn, H, DK, DV), jnp.float32)
        _, o = jax.lax.scan(step, S0, (tfirst(q), tfirst(k), tfirst(vf), tfirst(g), tfirst(beta)))
        o = jnp.moveaxis(o, 0, 1)
        g2 = (hidden_states @ Wga @ Wgb).reshape(Bn, Tn, H, DV).astype(jnp.float32)
        normed = o * jax.lax.rsqrt(jnp.mean(o * o, -1, keepdims=True) + EPS) * norm_w
        o = normed * jax.nn.sigmoid(g2)
        o = o.reshape(Bn, Tn, H * DV).astype(hidden_states.dtype)
        return o @ Wo

    def _L0_ffn_ref(x, W_up, W_gate, W_down):
        import jax, jax.numpy as jnp
        import numpy as np
        D_MODEL = 256
        D_EXPERT = 1024
        EPS = 1e-08

        def ternary_quant(w):
            scale = jnp.mean(jnp.abs(w)) + EPS
            q = jnp.clip(jnp.round(w / scale), -1.0, 1.0) * scale
            return w + jax.lax.stop_gradient(q - w)
        wu = ternary_quant(W_up)
        wg = ternary_quant(W_gate)
        wd = ternary_quant(W_down)
        up = jnp.einsum('bsd,ed->bse', x, wu)
        gate = jnp.einsum('bsd,ed->bse', x, wg)
        hidden = jax.nn.silu(up) * gate
        return jnp.einsum('bse,de->bsd', hidden, wd)
    x = L0_attn_hidden_states
    xn = _layernorm(x, axis=-1)
    x = x + _L0_attn_ref(xn, L0_attn_Wq, L0_attn_Wk, L0_attn_Wv, L0_attn_conv_q, L0_attn_conv_k, L0_attn_conv_v, L0_attn_A_log, L0_attn_Wfa, L0_attn_Wfb, L0_attn_dt_bias, L0_attn_Wb, L0_attn_Wga, L0_attn_Wgb, L0_attn_norm_w, L0_attn_Wo) + _L0_ffn_ref(xn, L0_ffn_W_up, L0_ffn_W_gate, L0_ffn_W_down)
    return x

_drawn_inputs = setup_inputs


def setup_inputs(seed=0):
    import zlib

    import numpy as np

    out = dict(_drawn_inputs(seed))
    spreads = {'L0_attn_dt_bias': (0.0, 0.8), 'L0_attn_norm_w': (1.0, 0.561)}
    factors = {'L0_attn_Wfa': 8.0,
     'L0_attn_Wfb': 8.0,
     'L0_attn_Wb': 3.111,
     'L0_attn_Wga': 8.0,
     'L0_attn_Wgb': 8.0}
    for name, (base, spread) in spreads.items():
        noise = np.random.default_rng([zlib.crc32(name.encode()), seed]).standard_normal(out[name].shape)
        drawn = base * np.exp(spread * noise) if base else spread * noise
        out[name] = jnp.asarray(drawn.astype(out[name].dtype))
    for name, factor in factors.items():
        out[name] = (out[name] * factor).astype(out[name].dtype)
    return out
```

```python
from contextlib import ExitStack

import numpy as np

import concourse.bass as bass
from concourse import mybir

F32 = mybir.dt.float32
U32 = mybir.dt.uint32
ALU = mybir.AluOpType
ACT = mybir.ActivationFunctionType
AX = mybir.AxisListType

P = 128
NB = 2
T = 256
TOK = NB * T
NC = TOK // P
HEADS = 16
HID = 256
KT = HID // P
EXP = 1024
ET = EXP // P
TAPS = 4
SB = 32
SMALL = (1, 2, 4, 8, 16)
NSMALL = len(SMALL)

W_F, W_K, W_Q, W_V = 0, 1, 3, 5
WCOLS = 7 * P
C_Q, C_K, C_V, C_DT, C_A, C_N = 0, 4, 8, 12, 13, 14

K_ID = 0
K_ID32 = K_ID + P
K_SM = K_ID32 + SB
K_M32 = K_SM + NSMALL * 16
K_OSC = K_M32 + 2
K_QSC = K_OSC + 1
K_HALF = K_QSC + 1
K_NHALF = K_HALF + 1 * NC
K_ONES = K_NHALF + 1 * NC
K_COLS = K_ONES + P

LN_EPS = 1e-5
QK_EPS = 4e-6
O_EPS = 1e-6


def constants():
    c = np.zeros((P, K_COLS), np.float32)
    i = np.arange(P)
    c[i, K_ID + i] = 1
    c[i, K_ID32 + i % SB] = 1
    for n, h in enumerate(SMALL):
        for j in range(16):
            t = (j // h) * 2 * h + h + j % h
            c[:, K_SM + 16 * n + j] = ((i % SB) // (2 * h) == t // (2 * h)) & ((i % SB) % (2 * h) < h)
    for p in range(2):
        c[:, K_M32 + p] = (i // SB == 2 * p)
    c[:, K_OSC] = 1.0 / P
    c[:, K_QSC] = P * O_EPS
    c[:, K_HALF:K_HALF + NC] = 0.5
    c[:, K_NHALF:K_NHALF + NC] = -0.5
    c[:, K_ONES:K_ONES + P] = 1.0
    return c


def build(nc, x_d, wh_d, wgb_d, sm_d, wfg_d, wb_d, wo_d, nw_d, wup_d, wgt_d, wdn_d, const_d, out_d):
    groups = x_d.shape[0]
    ctx = ExitStack()
    with ctx:
        def sb(name, shape, dt=F32):
            return ctx.enter_context(nc.sbuf_tensor(name, shape, dt))

        def bank(name):
            return ctx.enter_context(nc.psum_tensor(name, [P, 512], F32))

        cst = sb("cst", [P, K_COLS])
        smalls = sb("smalls", [P, HEADS, 16])
        wfg = sb("wfg", [P, 2, KT, P])
        wb = sb("wb", [P, KT, HEADS])
        wo = sb("wo", [P, HEADS, HID])
        nw = sb("nw", [P, 1])
        wup = sb("wup", [P, KT, EXP])
        wgt = sb("wgt", [P, KT, EXP])
        wdn = sb("wdn", [P, ET, HID])
        tern = sb("tern", [P, 2048])
        tern2 = sb("tern2", [P, 2048])
        wsum = sb("wsum", [P, 3])
        wscale = sb("wscale", [P, 3])
        wthr = sb("wthr", [P, 6])
        upscale = sb("upscale", [P, 1])
        hidscale = sb("hidscale", [P, 1])
        xt = sb("xt", [P, NC, HID])
        xn = sb("xn", [P, NC, HID])
        bst = sb("bst", [P, NC, 6])
        mv = sb("mv", [P, NC, 2])
        rstd = sb("rstd", [P, NC])
        xnT = sb("xnT", [P, KT, TOK])
        faT = sb("faT", [P, TOK])
        gaT = sb("gaT", [P, TOK])
        beta = sb("beta", [P, HEADS, NC])
        OG = sb("OG", [P, HEADS, TOK])
        hid = sb("hid", [P, ET, TOK])
        ftan = sb("ftan", [P, TOK])
        fu = sb("fu", [P, TOK])
        ot = sb("ot", [P, NC, HID])
        wh = sb("wh", [P, WCOLS])
        wgb = sb("wgb", [P, P])
        sm = sb("sm", [P, 16])
        acc = sb("acc", [P, 3, TOK])
        th = sb("th", [P, 3, TOK])
        gbuf = sb("gbuf", [P, TOK])
        kq = sb("kq", [P, 2, TOK])
        vv = sb("vv", [P, TOK])
        G = {1 << n: sb(f"G{1 << n}", [P, TOK >> n]) for n in range(7)}
        KQ = sb("KQ", [P, 2, TOK])
        KL = sb("KL", [P, TOK])
        ksq = sb("ksq", [P, TOK])
        qsq = sb("qsq", [P, TOK])
        ssk = sb("ssk", [P, NC])
        ssk4 = sb("ssk4", [P, NC])
        rec = sb("rec", [P, NC])
        b2 = sb("b2", [P, NC])
        b2n = sb("b2n", [P, NC])
        nh = sb("nh", [P, NC])
        mb = sb("mb", [P, NSMALL, NC, 16])
        mb32 = sb("mb32", [P, NC, 2])
        L = sb("L", [P, NSMALL, NC, SB])
        AQc = sb("AQc", [P, NC, SB])
        AQ = sb("AQ", [P, NC, P])
        AXc = sb("AXc", [P, NB, 2 * P])
        LT32 = sb("LT32", [P, NC, 2, SB])
        LT64 = sb("LT64", [P, NC, 64])
        TT = sb("TT", [P, NC, 2, SB])
        Ms = sb("Ms", [P, NC, SB])
        M64 = sb("M64", [P, NC, 64])
        Tf = sb("Tf", [P, NC, 64])
        TTf = sb("TTf", [P, NC, P])
        Vn = sb("Vn", [P, NC, P])
        R = sb("R", [P, NB, P])
        U = sb("U", [P, NC, P])
        sg = sb("sg", [P, TOK])
        OGr = sb("OGr", [P, TOK])
        osq = sb("osq", [P, TOK])
        st = sb("st", [P, NC])
        rr = sb("rr", [P, NC])

        bQ, bK, bV, bG, bA, bB, bC, bT = [bank(f"bank{i}") for i in range(8)]
        bconv = [bK, bQ, bV]

        S = {}

        PER_HEAD = {
            "PE": ["proj_g", "proj_k", "proj_q", "proj_v", "ssk_mm", "diag_mm", "vT_mm",
                   "lv1_mm", "lv2_mm", "lv4_mm", "lv8_mm", "lv16_mm", "lv32_mm", "lv64_mm", "lv128_mm",
                   "t1_mm", "m2_mm", "m4_mm", "m8_mm", "m16_mm", "t2_mm", "t4_mm", "t8_mm", "t16_mm",
                   "m32_mm", "t32_mm", "m64_mm", "t64_mm", "u0_mm", "x_mm", "u1_mm", "o_mm", "st_mm",
                   "rb_mm", "gg_mm"],
            "ACT": ["tap_k", "tap_q", "tap_v", "g_exp", "g_ln", "g_ready", "tanh_k", "tanh_q", "tanh_v",
                    "ksq_ok", "qsq_ok", "kl_odd", "v_norm", "q64_ok", "ax_ok",
                    "m2_ok", "m4_ok", "m8_ok", "m16_ok", "m32_ok", "m64_ok", "t64_ok",
                    "tf_ok", "aq_ok", "u0_ok", "u1_ok", "osq_ok", "sg_ok"],
            "DVE": ["g_min", "g_max"] + [f"cv{j}_{n}" for j in (1, 2, 3) for n in "kqv"]
                   + ["silu_k", "silu_q", "silu_v", "ssk_ok", "rec_ok", "b2_ok", "kq1", "kq2", "kq4", "kq8",
                      "kq16", "kq32", "kq64", "kq128", "a_diag", "a_q1", "a_q2", "a1_ok", "a_q8", "a2_ok", "a32_ok",
                      "k64_ok", "tt1", "tt2", "tt4", "tt8", "tt16", "t32_ok", "r_ok", "og_raw", "st_ok",
                      "og_ok"],
            "POOL": ["sm_ok", "kl2", "kl4", "kl8", "kl16", "kl32", "kl64", "kl128", "nh_ok", "mb_ok",
                     "rr_ok"] + [f"gg{1 << n}" for n in range(1, 7)],
        }
        PER_GROUP = {
            "PE": ["xT_mm", "fg_mm", "beta_mm", "group_mm"],
            "ACT": ["xT_ok", "fa_ok", "ga_ok", "beta_exp"],
            "DVE": ["bn_ok", "mv_ok", "xn_ok", "beta_1", "beta_ok", "out_ok"],
            "POOL": ["rstd_ok"],
        }

        ONCE = ["const_in", "x_in", "w_in", "wgb_in", "out_done", "wsum_ok", "wsum_mm", "zero_ok", "setup_v",
                "setup_ok", "a_exp", "rstd_e", "ffn_mm", "ffn_tanh", "ffn_u", "ffn_hid"]
        for names in (*PER_HEAD.values(), *PER_GROUP.values(), ONCE):
            for name in names:
                S[name] = ctx.enter_context(nc.semaphore(name))

        def prime(eng, who):
            for name in PER_HEAD[who] + PER_GROUP[who]:
                eng.sem_inc(S[name], 1)

        class Unit:
            def __init__(self, eng, n):
                self.n = n
                self.now = n + 2 if isinstance(n, int) else eng.snap(n + 2)
                self.before = n + 1 if isinstance(n, int) else eng.snap(n + 1)
                self.dma = 16 * n + 16 if isinstance(n, int) else eng.snap(n * 16 + 16)
                if not isinstance(n, int):
                    eng.compute_val(self.now)
                    eng.compute_val(self.before)
                    if eng in (nc.sync, nc.tensor):
                        eng.compute_val(self.dma)

        def now(eng, u, *names):
            for n in names:
                eng.wait_ge(S[n], u.now)

        def before(eng, u, *names):
            for n in names:
                eng.wait_ge(S[n], u.before)

        def constant_wait(eng):
            eng.wait_ge(S["setup_ok"], 1)

        def halves(ap, h):
            d = " ".join(f"a{i}" for i in range(len(ap.shape) - 1))
            return ap.rearrange(f"{d} (n two h) -> {d} n two h", two=2, h=h)

        def const(c0, n):
            return cst[:, c0:c0 + n]

        block = ctx.enter_context(nc.Block())

        @block.sync
        def _(sp):
            sp.sem_inc(S["out_done"], 16)
            for dst, src in ((cst[:, :], const_d), (wup[:, :, :], wup_d), (wgt[:, :, :], wgt_d),
                             (wdn[:, :, :], wdn_d), (smalls[:, :, :], sm_d), (wfg[:, :, :, :], wfg_d),
                             (wb[:, :, :], wb_d), (wo[:, :, :], wo_d), (nw[:, :], nw_d)):
                sp.dma_start(dst, src).then_inc(S["const_in"], 16)

            def load_x(g, gu):
                sp.wait_ge(S["out_done"], gu.dma)
                before(sp, gu, "out_ok")
                sp.dma_start(xt[:, :, :], x_d[g]).then_inc(S["x_in"], 16)

            def load_w(u, h):
                before(sp, u, "proj_v")
                sp.dma_start(wh[:, :], wh_d[h]).then_inc(S["w_in"], 16)

            def load_wgb(u, h):
                before(sp, u, "gg_mm")
                sp.dma_start(wgb[:, :], wgb_d[h]).then_inc(S["wgb_in"], 16)

            with sp.Fori(0, groups) as g:
                gu = Unit(sp, g)
                load_x(g, gu)
                load_w(Unit(sp, g * HEADS), 0)
                with sp.Fori(0, HEADS - 1) as h:
                    load_wgb(Unit(sp, g * HEADS + h), h)
                    load_w(Unit(sp, g * HEADS + h + 1), h + 1)
                load_wgb(Unit(sp, g * HEADS + HEADS - 1), HEADS - 1)
                now(sp, gu, "out_ok")
                sp.dma_start(out_d[g], ot[:, :, :]).then_inc(S["out_done"], 16)
            sp.wait_ge(S["out_done"], 16 * groups + 16)

        @block.tensor
        def _(pe):
            mm = nc.tensor.matmul
            prime(pe, "PE")

            def proj(u):
                pe.wait_ge(S["w_in"], u.dma)
                before(pe, u, "g_max")
                mm(bG[:, :], wh[:, W_F * P:(W_F + 1) * P], faT[:, :], start=True, stop=True).then_inc(S["proj_g"], 1)
                for bnk, w0, name, free in ((bK, W_K, "proj_k", "cv3_k"), (bQ, W_Q, "proj_q", "cv3_q"),
                                            (bV, W_V, "proj_v", "cv3_v")):
                    before(pe, u, free)
                    for t in range(KT):
                        last = mm(bnk[:, :], wh[:, (w0 + t) * P:(w0 + t + 1) * P], xnT[:, t, :],
                                  start=(t == 0), stop=(t == KT - 1))
                    last.then_inc(S[name], 1)

            def norms(u):
                now(pe, u, "ksq_ok")
                before(pe, u, "og_ok")
                for c in range(NC):
                    last = mm(bB[:, c:c + 1], ksq[:, c * P:(c + 1) * P], const(K_ONES, 1), start=True, stop=True)
                last.then_inc(S["ssk_mm"], 1)
                now(pe, u, "silu_k", "silu_q")
                before(pe, u, "sg_ok")
                for c in range(NC):
                    for q in range(4):
                        t0 = c * P + q * SB
                        last = mm(bA[q * SB:(q + 1) * SB, 384 + c * SB:384 + (c + 1) * SB],
                                  kq[:, 0, t0:t0 + SB], kq[:, 1, t0:t0 + SB], start=True, stop=True)
                last.then_inc(S["diag_mm"], 1)

            def v_turn(u):
                now(pe, u, "silu_v")
                before(pe, u, "u1_ok")
                for c in range(NC):
                    last = nc.tensor.transpose(bT[:, c * P:(c + 1) * P], vv[:, c * P:(c + 1) * P], const(K_ID, P))
                last.then_inc(S["vT_mm"], 1)

            def small_level(u, h):
                n = SMALL.index(h)
                bnk, col = (bA, n * P) if h <= 4 else (bB, (n - 3) * P)
                left = kq[:, 0, :] if h == 1 else KL[:, :]
                now(pe, u, f"kq{h}")
                if h > 1:
                    now(pe, u, f"kl{h}")
                if h == 2:
                    now(pe, u, "kl_odd")
                if h == 8:
                    now(pe, u, "ssk_ok")
                for c in range(NC):
                    for q in range(4):
                        t0 = c * P + q * SB
                        right = halves(KQ[:, :, t0:t0 + SB], h)[:, :, :, 1, :]
                        o = bnk[q * SB:(q + 1) * SB, col + c * SB:col + (c + 1) * SB]
                        last = mm(o.rearrange("p (k n h) -> p k n h", k=2, h=h), left[:, t0:t0 + SB], right,
                                  start=True, stop=True)
                last.then_inc(S[f"lv{h}_mm"], 1)

            def level32(u):
                now(pe, u, "kq32", "kl32")
                before(pe, u, "og_raw")
                for c in range(NC):
                    right = halves(KQ[:, :, c * P:(c + 1) * P], SB)[:, :, :, 1, :]
                    last = mm(bC[:, c * P:(c + 1) * P].rearrange("p (k n h) -> p k n h", k=2, h=SB),
                              KL[:, c * P:(c + 1) * P], right, start=True, stop=True)
                last.then_inc(S["lv32_mm"], 1)

            def level64(u):
                now(pe, u, "kq64", "kl64", "a1_ok")
                for c in range(NC):
                    last = mm(bA[0:64, c * P:(c + 1) * P].rearrange("p (k h) -> p k h", k=2),
                              KL[:, c * P:c * P + 64], KQ[:, :, c * P + 64:(c + 1) * P], start=True, stop=True)
                last.then_inc(S["lv64_mm"], 1)

            def level128(u):
                now(pe, u, "kq128", "kl128", "a2_ok")
                for b in range(NB):
                    last = mm(bB[:, b * T:(b + 1) * T].rearrange("p (k h) -> p k h", k=2),
                              KL[:, b * T:b * T + P], KQ[:, :, b * T + P:(b + 1) * T], start=True, stop=True)
                last.then_inc(S["lv128_mm"], 1)

            def inv_first(u):
                constant_wait(pe)
                now(pe, u, "a1_ok", "v_norm")
                for c in range(NC):
                    for q in range(4):
                        r = slice(q * SB, (q + 1) * SB)
                        last = mm(bT[r, c * SB:(c + 1) * SB], L[r, 0, c, :], cst[r, K_ID32:K_ID32 + SB],
                                  start=True, stop=True)
                last.then_inc(S["t1_mm"], 1)

            def inv_m(u, h):
                n = SMALL.index(h)
                constant_wait(pe)
                now(pe, u, "a2_ok" if h >= 8 else "a1_ok", f"tt{h // 2}")
                for c in range(NC):
                    for q in range(4):
                        r = slice(q * SB, (q + 1) * SB)
                        last = mm(bT[r, c * SB:(c + 1) * SB], L[r, n, c, :], TT[r, c, 0, :], start=True, stop=True)
                last.then_inc(S[f"m{h}_mm"], 1)

            def inv_t(u, h):
                constant_wait(pe)
                now(pe, u, f"m{h}_ok")
                for c in range(NC):
                    for q in range(4):
                        r = slice(q * SB, (q + 1) * SB)
                        o = P + c * 2 * SB
                        mm(bT[r, o:o + SB], TT[r, c, 1, :], Ms[r, c, :], start=True, stop=True)
                        last = mm(bT[r, o + SB:o + 2 * SB], Ms[r, c, :], TT[r, c, 1, :], start=True, stop=True)
                last.then_inc(S[f"t{h}_mm"], 1)

            def inv32(u):
                constant_wait(pe)
                now(pe, u, "a32_ok", "tt16")
                for c in range(NC):
                    for p in range(2):
                        lo, hi = slice(64 * p, 64 * p + SB), slice(64 * p + SB, 64 * p + 64)
                        last = mm(bT[hi, c * SB:(c + 1) * SB], LT32[lo, c, p, :], TT[lo, c, 0, :], start=True, stop=True)
                last.then_inc(S["m32_mm"], 1)
                constant_wait(pe)
                now(pe, u, "m32_ok")
                for c in range(NC):
                    for p in range(2):
                        lo, hi = slice(64 * p, 64 * p + SB), slice(64 * p + SB, 64 * p + 64)
                        o = slice(P + c * SB, P + (c + 1) * SB)
                        mm(bT[hi, o], TT[hi, c, 1, :], Ms[hi, c, :], start=True, stop=True)
                        last = mm(bT[lo, o], Ms[hi, c, :], TT[hi, c, 1, :], start=True, stop=True)
                last.then_inc(S["t32_mm"], 1)

            def inv64(u):
                constant_wait(pe)
                now(pe, u, "k64_ok", "t32_ok", "tf_ok")
                for c in range(NC):
                    last = mm(bT[64:128, c * 64:(c + 1) * 64], LT64[0:64, c, :], Tf[0:64, c, :], start=True, stop=True)
                last.then_inc(S["m64_mm"], 1)
                constant_wait(pe)
                now(pe, u, "m64_ok")
                for c in range(NC):
                    last = mm(bT[0:64, c * 64:(c + 1) * 64], M64[64:128, c, :], TTf[64:128, c, 64:128],
                              start=True, stop=True)
                last.then_inc(S["t64_mm"], 1)

            def solve(u):
                now(pe, u, "t64_ok")
                for b in range(NB):
                    last = mm(bT[:, b * P:(b + 1) * P], TTf[:, 2 * b, :], Vn[:, 2 * b, :], start=True, stop=True)
                last.then_inc(S["u0_mm"], 1)
                now(pe, u, "u0_ok", "ax_ok")
                for b in range(NB):
                    last = mm(bT[:, (2 + b) * P:(3 + b) * P], AXc[:, b, 0:P], U[:, 2 * b, :], start=True, stop=True)
                last.then_inc(S["x_mm"], 1)
                now(pe, u, "r_ok")
                for b in range(NB):
                    last = mm(bT[:, b * P:(b + 1) * P], TTf[:, 2 * b + 1, :], R[:, b, :], start=True, stop=True)
                last.then_inc(S["u1_mm"], 1)

            def output(u):
                now(pe, u, "u1_ok", "aq_ok", "q64_ok", "a32_ok")
                for b in range(NB):
                    c0, c1 = 2 * b, 2 * b + 1
                    mm(bC[:, c0 * P:(c0 + 1) * P], U[:, c0, :], AQ[:, c0, :], start=True, stop=True)
                    mm(bC[:, c1 * P:(c1 + 1) * P], U[:, c0, :], AXc[:, b, P:2 * P], start=True, stop=False)
                    last = mm(bC[:, c1 * P:(c1 + 1) * P], U[:, c1, :], AQ[:, c1, :], start=False, stop=True)
                last.then_inc(S["o_mm"], 1)

            def gate2(u):
                pe.wait_ge(S["wgb_in"], u.dma)
                now(pe, u, "q64_ok", "k64_ok")
                mm(bA[:, :], wgb[:, :], gaT[:, :], start=True, stop=True).then_inc(S["gg_mm"], 1)

            def scale_out(u):
                now(pe, u, "osq_ok", "ax_ok")
                for c in range(NC):
                    mm(bB[:, c:c + 1], osq[:, c * P:(c + 1) * P], const(K_OSC, 1), start=True, stop=False)
                    last = mm(bB[:, c:c + 1], qsq[:, c * P:(c + 1) * P], const(K_QSC, 1), start=False, stop=True)
                last.then_inc(S["st_mm"], 1)
                now(pe, u, "rr_ok")
                for c in range(NC):
                    last = mm(bB[:, c * P:(c + 1) * P], rr[:, c:c + 1].to_broadcast([P, P]), const(K_ID, P),
                              start=True, stop=True)
                last.then_inc(S["rb_mm"], 1)

            def attend(u):
                norms(u)
                small_level(u, 1)
                v_turn(u)
                for h in SMALL[1:]:
                    small_level(u, h)
                level32(u)
                level64(u)
                level128(u)
                inv_first(u)
                for h in SMALL[1:]:
                    inv_m(u, h)
                    inv_t(u, h)
                inv32(u)
                inv64(u)
                gate2(u)
                solve(u)
                output(u)
                scale_out(u)

            def group_in(gu):
                now(pe, gu, "xn_ok")
                before(pe, gu, "out_ok")
                for c in range(NC):
                    for t in range(KT):
                        last = nc.tensor.transpose((bQ, bK)[t][:, c * P:(c + 1) * P], xn[:, c, t * P:(t + 1) * P],
                                                   const(K_ID, P))
                last.then_inc(S["xT_mm"], 1)
                now(pe, gu, "xT_ok")
                for i, bnk in enumerate((bV, bG)):
                    for t in range(KT):
                        last = mm(bnk[:, :], wfg[:, i, t, :], xnT[:, t, :], start=(t == 0), stop=(t == KT - 1))
                last.then_inc(S["fg_mm"], 1)
                for c in range(NC):
                    for t in range(KT):
                        last = mm(bA[:, c * HEADS:(c + 1) * HEADS], xnT[:, t, c * P:(c + 1) * P], wb[:, t, :],
                                  start=(t == 0), stop=(t == KT - 1))
                last.then_inc(S["beta_mm"], 1)
                now(pe, gu, "fa_ok", "ga_ok", "beta_exp")

            def group_out(g, gu):
                now(pe, Unit(pe, g * HEADS + HEADS - 1), "cv3_k", "cv3_q")
                for e in range(ET):
                    e0 = e * P
                    if e >= 1:
                        pe.wait_ge(S["ffn_hid"], g * ET + e)
                    for bnk, w in ((bQ, wup), (bK, wgt)):
                        for t in range(KT):
                            last = mm(bnk[:, :], w[:, t, e0:e0 + P], xnT[:, t, :], start=(t == 0), stop=(t == KT - 1))
                    last.then_inc(S["ffn_mm"], 1)
                pe.wait_ge(S["ffn_hid"], g * ET + ET)
                now(pe, Unit(pe, g * HEADS + HEADS - 1), "og_ok")
                for c in range(NC):
                    o = (bV, bG)[c // 2][:, (c % 2) * HID:(c % 2 + 1) * HID]
                    for h in range(HEADS):
                        mm(o, OG[:, h, c * P:(c + 1) * P], wo[:, h, :], start=(h == 0), stop=False)
                    for e in range(ET):
                        last = mm(o, hid[:, e, c * P:(c + 1) * P], wdn[:, e, :], start=False, stop=(e == ET - 1))
                last.then_inc(S["group_mm"], 1)

            pe.wait_ge(S["const_in"], 16 * 9)
            pe.wait_ge(S["wsum_ok"], 3)
            mm(bQ[:, 0:3], const(K_ONES, P), wsum[:, :], start=True, stop=True).then_inc(S["wsum_mm"], 1)
            pe.wait_ge(S["setup_ok"], 1)
            with pe.Fori(0, groups) as g:
                gu = Unit(pe, g)
                group_in(gu)
                proj(Unit(pe, g * HEADS))
                with pe.Fori(0, HEADS - 1) as h:
                    attend(Unit(pe, g * HEADS + h))
                    proj(Unit(pe, g * HEADS + h + 1))
                attend(Unit(pe, g * HEADS + HEADS - 1))
                group_out(g, gu)

        @block.scalar
        def _(act):
            A = nc.scalar.activation
            prime(act, "ACT")

            def taps(u):
                now(act, u, "sm_ok")
                for i, (n, c0) in enumerate((("k", C_K), ("q", C_Q), ("v", C_V))):
                    now(act, u, f"proj_{n}")
                    before(act, u, f"silu_{n}")
                    A(acc[:, i, :], bconv[i][:, :], ACT.Copy, scale=sm[:, c0 + 3:c0 + 4])\
                        .then_inc(S[f"tap_{n}"], 1)

            def gates(u):
                now(act, u, "g_min")
                A(gbuf[:, :], gbuf[:, :], ACT.Exp).then_inc(S["g_exp"], 1)
                now(act, u, "g_exp")
                A(gbuf[:, :], gbuf[:, :], ACT.Ln, bias=1.0).then_inc(S["g_ln"], 1)
                now(act, u, "g_max")
                before(act, u, "kq1", "kq2", "kl2", "gg2")
                A(G[1][:, :], gbuf[:, :], ACT.Exp, scale=sm[:, C_A:C_A + 1]).then_inc(S["g_ready"], 1)

            def tanhs(u):
                for i, n in enumerate("kqv"):
                    now(act, u, f"cv3_{n}")
                    before(act, u, f"silu_{n}")
                    A(th[:, i, :], acc[:, i, :], ACT.Tanh, scale=0.5).then_inc(S[f"tanh_{n}"], 1)

            def squares(u):
                now(act, u, "silu_k")
                before(act, u, "ssk_mm")
                A(ksq[:, :], kq[:, 0, :], ACT.Square).then_inc(S["ksq_ok"], 1)
                before(act, u, "lv128_mm")
                A(halves(KL[:, :], 1)[:, :, 1, :], halves(kq[:, 0, :], 1)[:, :, 1, :], ACT.Copy).then_inc(S["kl_odd"], 1)
                now(act, u, "silu_q")
                before(act, u, "st_mm")
                A(qsq[:, :], kq[:, 1, :], ACT.Square).then_inc(S["qsq_ok"], 1)

            def v_norm(u):
                now(act, u, "nh_ok", "vT_mm")
                before(act, u, "u0_mm", "r_ok")
                for c in range(NC):
                    last = A(Vn[:, c, :], bT[:, c * P:(c + 1) * P], ACT.Copy, scale=nh[:, c:c + 1])
                last.then_inc(S["v_norm"], 1)

            def inv_small(u, h):
                now(act, u, f"m{h}_mm")
                A(Ms[:, :, :], bT[:, 0:P].rearrange("p (c s) -> p c s", c=NC), ACT.Copy).then_inc(S[f"m{h}_ok"], 1)

            def inv_big(u):
                now(act, u, "m32_mm")
                for p in range(2):
                    r = slice(64 * p + SB, 64 * p + 64)
                    last = A(Ms[r, :, :], bT[r, 0:P].rearrange("p (c s) -> p c s", c=NC), ACT.Copy)
                last.then_inc(S["m32_ok"], 1)

            def inv_64(u):
                now(act, u, "m64_mm")
                A(M64[64:128, :, :], bT[64:128, 0:256].rearrange("p (c s) -> p c s", c=NC), ACT.Copy)\
                    .then_inc(S["m64_ok"], 1)
                now(act, u, "t64_mm")
                A(TTf[0:64, :, 64:128], bT[0:64, 0:256].rearrange("p (c s) -> p c s", c=NC), ACT.Copy)\
                    .then_inc(S["t64_ok"], 1)

            def big_levels(u):
                now(act, u, "lv64_mm", "k64_ok")
                before(act, u, "o_mm")
                A(AQ[0:64, :, 64:128],
                  bA[0:64, :].rearrange("p (c k s) -> p c k s", c=NC, k=2)[:, :, 1, :], ACT.Copy)\
                    .then_inc(S["q64_ok"], 1)
                now(act, u, "lv128_mm")
                A(AXc[:, :, :], bB[:, :].rearrange("p (b s) -> p b s", b=NB), ACT.Copy).then_inc(S["ax_ok"], 1)

            def place_aq(u):
                now(act, u, "a2_ok", "a32_ok")
                before(act, u, "o_mm")
                for q in range(4):
                    r = slice(q * SB, (q + 1) * SB)
                    last = A(AQ[r, :, r], AQc[r, :, :], ACT.Copy)
                last.then_inc(S["aq_ok"], 1)

            def place_t(u):
                now(act, u, "tt16")
                before(act, u, "u1_mm", "m64_mm")
                for q in range(4):
                    r = slice(q * SB, (q + 1) * SB)
                    A(TTf[r, :, r], TT[r, :, 1, :], ACT.Copy)
                    last = A(Tf[r, :, (q % 2) * SB:(q % 2 + 1) * SB], TT[r, :, 0, :], ACT.Copy)
                last.then_inc(S["tf_ok"], 1)

            def solve(u):
                now(act, u, "u0_mm", "b2_ok")
                before(act, u, "o_mm")
                for b in range(NB):
                    c = 2 * b
                    last = A(U[:, c, :], bT[:, b * P:(b + 1) * P], ACT.Copy, scale=b2[:, c:c + 1])
                last.then_inc(S["u0_ok"], 1)
                now(act, u, "u1_mm")
                for b in range(NB):
                    c = 2 * b + 1
                    last = A(U[:, c, :], bT[:, b * P:(b + 1) * P], ACT.Copy, scale=b2[:, c:c + 1])
                last.then_inc(S["u1_ok"], 1)

            def gate2(u):
                now(act, u, "gg_mm")
                before(act, u, "og_raw")
                A(sg[:, :], bA[:, :], ACT.Tanh, scale=0.5).then_inc(S["sg_ok"], 1)

            def out_sq(u):
                now(act, u, "o_mm")
                before(act, u, "st_mm")
                A(osq[:, :], bC[:, :], ACT.Square).then_inc(S["osq_ok"], 1)

            def attend(u):
                squares(u)
                v_norm(u)
                place_aq(u)
                big_levels(u)
                for h in SMALL[1:]:
                    inv_small(u, h)
                place_t(u)
                inv_big(u)
                inv_64(u)
                gate2(u)
                solve(u)
                out_sq(u)

            def project(u):
                taps(u)
                gates(u)
                tanhs(u)

            act.wait_ge(S["const_in"], 16 * 9)
            for i, w in enumerate((wup, wgt, wdn)):
                if i:
                    act.wait_ge(S["wsum_ok"], i)
                A(tern[:, :], w[:, :, :].rearrange("p a b -> p (a b)"), ACT.Abs,
                  accum_out=wsum[:, i:i + 1]).then_inc(S["wsum_ok"], 1)
            A(smalls[:, :, C_A], smalls[:, :, C_A], ACT.Exp).then_inc(S["a_exp"], 1)

            act.wait_ge(S["setup_ok"], 1)
            with act.Fori(0, groups) as g:
                gu = Unit(act, g)
                now(act, gu, "xT_mm")
                for t in range(KT):
                    last = A(xnT[:, t, :], (bQ, bK)[t][:, :], ACT.Copy)
                last.then_inc(S["xT_ok"], 1)
                now(act, gu, "fg_mm")
                A(faT[:, :], bV[:, :], ACT.Copy).then_inc(S["fa_ok"], 1)
                A(gaT[:, :], bG[:, :], ACT.Copy).then_inc(S["ga_ok"], 1)
                now(act, gu, "beta_mm")
                before(act, Unit(act, g * HEADS), "b2_ok")
                A(beta[:, :, :].rearrange("p h c -> p c h"), bA[:, 0:HEADS * NC].rearrange("p (c h) -> p c h", c=NC),
                  ACT.Exp, scale=-1.0).then_inc(S["beta_exp"], 1)
                project(Unit(act, g * HEADS))
                with act.Fori(0, HEADS - 1) as h:
                    attend(Unit(act, g * HEADS + h))
                    project(Unit(act, g * HEADS + h + 1))
                attend(Unit(act, g * HEADS + HEADS - 1))
                for e in range(ET):
                    act.wait_ge(S["ffn_mm"], g * ET + e + 1)
                    if e:
                        act.wait_ge(S["ffn_hid"], g * ET + e)
                    A(ftan[:, :], bQ[:, :], ACT.Tanh, scale=upscale[:, 0:1]).then_inc(S["ffn_tanh"], 1)

        @block.vector
        def _(ve):
            TT2 = nc.vector.tensor_tensor
            TS = nc.vector.tensor_scalar
            STT = nc.vector.scalar_tensor_tensor
            prime(ve, "DVE")

            def gate_min(u):
                now(ve, u, "sm_ok", "proj_g")
                before(ve, u, "g_ready")
                TS(gbuf[:, :], bG[:, :], sm[:, C_DT:C_DT + 1], 40.0, ALU.add, ALU.min).then_inc(S["g_min"], 1)

            def gate_max(u):
                now(ve, u, "g_ln")
                STT(gbuf[:, :], bG[:, :], sm[:, C_DT:C_DT + 1], gbuf[:, :], ALU.add, ALU.max).then_inc(S["g_max"], 1)

            def conv(u, j):
                for i, (n, c0) in enumerate((("k", C_K), ("q", C_Q), ("v", C_V))):
                    now(ve, u, f"tap_{n}" if j == 1 else f"cv{j - 1}_{n}")
                    a = acc[:, i, :].rearrange("p (b t) -> p b t", b=NB)[:, :, j:T]
                    s = bconv[i][:, :].rearrange("p (b t) -> p b t", b=NB)[:, :, 0:T - j]
                    STT(a, s, sm[:, c0 + 3 - j:c0 + 4 - j], a, ALU.mult, ALU.add).then_inc(S[f"cv{j}_{n}"], 1)

            def silu(u, i):
                n = "kqv"[i]
                now(ve, u, f"tanh_{n}")
                if i == 0:
                    before(ve, u, "diag_mm", "lv1_mm", "kq1", "kl2", "kl_odd", "ksq_ok")
                elif i == 1:
                    before(ve, u, "diag_mm", "kq1", "qsq_ok")
                else:
                    before(ve, u, "vT_mm")
                dst = vv[:, :] if i == 2 else kq[:, i, :]
                STT(dst, th[:, i, :], 1.0, acc[:, i, :], ALU.add, ALU.mult).then_inc(S[f"silu_{n}"], 1)

            def first(u):
                now(ve, u, "g_ready", "silu_k", "silu_q")
                before(ve, u, "lv128_mm")
                TT2(KQ[:, :, :], kq[:, :, :], G[1][:, :].unsqueeze(1).to_broadcast([P, 2, TOK]), ALU.mult)\
                    .then_inc(S["kq1"], 1)

            def norms(u, h):
                now(ve, u, "ssk_mm")
                before(ve, u, "nh_ok")
                TS(ssk[:, :], bB[:, 0:NC], QK_EPS, None, ALU.add)
                TS(ssk4[:, :], bB[:, 0:NC], QK_EPS, 0.25, ALU.add, ALU.mult).then_inc(S["ssk_ok"], 1)
                now(ve, u, "ssk_ok")
                nc.vector.reciprocal(rec[:, :], ssk[:, :]).then_inc(S["rec_ok"], 1)
                now(ve, u, "rec_ok")
                before(ve, u, "u1_ok", "mb_ok", "k64_ok")
                TT2(b2[:, :], beta[:, h, :], rec[:, :], ALU.mult)
                STT(b2n[:, :], beta[:, h, :], -1.0, rec[:, :], ALU.mult, ALU.mult).then_inc(S["b2_ok"], 1)

            def up(u, h):
                now(ve, u, f"lv{h}_mm", f"kq{h}")
                if h > 1:
                    now(ve, u, f"gg{h}")
                if h < 64:
                    o = halves(KQ[:, :, :], h)[:, :, :, 1, :]
                    g = halves(G[h][:, :], 1)[:, :, 0, :]
                    g = g.unsqueeze(1).to_broadcast([P, 2, TOK // (2 * h), h])
                else:
                    o = KQ[:, :, :].rearrange("p k (b f t) -> p k b f t", b=NB, f=4)[:, :, :, 3, :]
                    g = G[64][:, :].rearrange("p (b f) -> p b f", b=NB)[:, :, 2:3]
                    g = g.unsqueeze(1).to_broadcast([P, 2, NB, 64])
                TT2(o, o, g, ALU.mult).then_inc(S[f"kq{2 * h}"], 1)

            def small_masks(u, lot):
                now(ve, u, "lv4_mm" if lot == 0 else "lv16_mm", "mb_ok", "diag_mm")
                before(ve, u, "m16_mm", "t1_mm", "aq_ok")
                if lot == 0:
                    TT2(AQc[:, :, :], bA[:, 384:512].rearrange("p (c s) -> p c s", c=NC),
                        const(K_ID32, SB).unsqueeze(1).to_broadcast([P, NC, SB]), ALU.mult).then_inc(S["a_diag"], 1)
                for h in ((1, 2, 4) if lot == 0 else (8, 16)):
                    n = SMALL.index(h)
                    bnk, col = (bA, n * P) if lot == 0 else (bB, (n - 3) * P)
                    src = bnk[:, col:col + P].rearrange("p (c k n h) -> p c k n h", c=NC, k=2, h=h)
                    dst = halves(L[:, n, :, :], h)[:, :, :, 1, :]
                    m = mb[:, n, :, :].rearrange("p c (n h) -> p c n h", h=h)
                    TT2(dst, src[:, :, 0, :, :], m, ALU.mult)
                    constant_wait(ve)
                    now(ve, u, {1: "a_diag", 2: "a_q1", 4: "a_q2", 8: "a1_ok", 16: "a_q8"}[h])
                    m = const(K_SM + 16 * n, 16).bitcast(U32).rearrange("p (n h) -> p n h", h=h)\
                        .unsqueeze(1).to_broadcast([P, NC, 16 // h, h])
                    sem = {1: "a_q1", 2: "a_q2", 4: "a1_ok", 8: "a_q8", 16: "a2_ok"}[h]
                    nc.vector.copy_predicated(halves(AQc[:, :, :], h)[:, :, :, 1, :], m, src[:, :, 1, :, :])\
                        .then_inc(S[sem], 1)

            def masks32(u):
                now(ve, u, "lv32_mm", "mb_ok")
                before(ve, u, "m32_mm", "o_mm", "aq_ok")
                src = bC[:, :].rearrange("p (c k n h) -> p c k n h", c=NC, k=2, n=2)
                TT2(LT32[:, :, :, :], src[:, :, 0, :, :], mb32[:, :, :].unsqueeze(3).to_broadcast([P, NC, 2, SB]),
                    ALU.mult)
                TT2(halves(AQ[:, :, :], SB)[:, :, :, 1, :], src[:, :, 1, :, :],
                    const(K_M32, 2).unsqueeze(1).unsqueeze(3).to_broadcast([P, NC, 2, SB]), ALU.mult)\
                    .then_inc(S["a32_ok"], 1)

            def masks64(u):
                now(ve, u, "lv64_mm", "b2_ok")
                before(ve, u, "m64_mm")
                TT2(LT64[0:64, :, :], bA[0:64, :].rearrange("p (c k s) -> p c k s", c=NC, k=2)[:, :, 0, :],
                    b2n[0:64, :].unsqueeze(2).to_broadcast([64, NC, 64]), ALU.mult).then_inc(S["k64_ok"], 1)

            def inv_first(u):
                now(ve, u, "t1_mm")
                before(ve, u, "t32_mm", "tf_ok")
                idc = const(K_ID32, SB).unsqueeze(1).to_broadcast([P, NC, SB])
                TT2(TT[:, :, 0, :], bT[:, 0:P].rearrange("p (c s) -> p c s", c=NC), idc, ALU.add)
                TT2(TT[:, :, 1, :], L[:, 0, :, :], idc, ALU.add).then_inc(S["tt1"], 1)

            def inv_add(u, h):
                now(ve, u, f"t{h}_mm")
                TT2(TT[:, :, :, :], bT[:, P:3 * P].rearrange("p (c k s) -> p c k s", c=NC, k=2), TT[:, :, :, :],
                    ALU.add).then_inc(S[f"tt{h}"], 1)

            def inv_32(u):
                now(ve, u, "t32_mm")
                before(ve, u, "u1_mm")
                src = bT[:, P:2 * P].rearrange("p (c s) -> p c s", c=NC)
                for p in range(2):
                    lo, hi = slice(64 * p, 64 * p + SB), slice(64 * p + SB, 64 * p + 64)
                    nc.vector.tensor_copy(Tf[hi, :, 0:SB], src[hi])
                    last = nc.vector.tensor_copy(TTf[lo, :, 64 * p + SB:64 * p + 64], src[lo])
                last.then_inc(S["t32_ok"], 1)

            def cross(u):
                now(ve, u, "x_mm", "v_norm")
                TT2(R[:, :, :], Vn[:, :, :].rearrange("p (b two) v -> p b two v", two=2)[:, :, 1, :],
                    bT[:, 2 * P:4 * P].rearrange("p (b v) -> p b v", b=NB), ALU.subtract).then_inc(S["r_ok"], 1)

            def finish(u, h):
                now(ve, u, "osq_ok", "sg_ok")
                STT(OGr[:, :], sg[:, :], 1.0, bC[:, :], ALU.add, ALU.mult).then_inc(S["og_raw"], 1)
                now(ve, u, "st_mm")
                before(ve, u, "rr_ok")
                TS(st[:, :], bB[:, 0:NC], P * O_EPS * QK_EPS, None, ALU.add).then_inc(S["st_ok"], 1)
                now(ve, u, "rb_mm", "og_raw")
                TT2(OG[:, h, :], OGr[:, :], bB[:, :], ALU.mult).then_inc(S["og_ok"], 1)

            def project(u):
                gate_min(u)
                conv(u, 1)
                gate_max(u)
                conv(u, 2)
                conv(u, 3)
                for i in range(3):
                    silu(u, i)

            def attend(u, h):
                first(u)
                norms(u, h)
                for l in (1, 2):
                    up(u, l)
                up(u, 4)
                small_masks(u, 0)
                up(u, 8)
                up(u, 16)
                small_masks(u, 1)
                up(u, 32)
                masks32(u)
                up(u, 64)
                masks64(u)
                inv_first(u)
                for l in SMALL[1:]:
                    inv_add(u, l)
                inv_32(u)
                cross(u)
                finish(u, h)

            for t in (L, TTf, Tf, AQ):
                last = nc.vector.memset(t[:], 0.0)
            last.then_inc(S["zero_ok"], 1)
            ve.wait_ge(S["wsum_ok"], 3)
            ve.wait_ge(S["wsum_mm"], 1)
            ve.wait_ge(S["zero_ok"], 1)
            TS(wscale[:, :], bQ[:, 0:3], 1.0 / (HID * EXP), 1e-8, ALU.mult, ALU.add).then_inc(S["setup_v"], 1)
            ve.wait_ge(S["setup_v"], 1)
            TS(wthr[:, 0:3], wscale[:, :], 0.5, None, ALU.mult)
            TS(wthr[:, 3:6], wscale[:, :], -0.5, None, ALU.mult).then_inc(S["setup_v"], 1)
            ve.wait_ge(S["setup_v"], 2)
            n = 2
            for i, w in enumerate((wup, wgt, wdn)):
                flat = w[:, :, :].rearrange("p a b -> p (a b)")
                TS(tern[:, :], flat, wthr[:, i:i + 1], None, ALU.is_gt)
                TS(tern2[:, :], flat, wthr[:, 3 + i:4 + i], None, ALU.is_lt).then_inc(S["setup_v"], 1)
                n += 1
                ve.wait_ge(S["setup_v"], n)
                TT2(flat, tern[:, :], tern2[:, :], ALU.subtract).then_inc(S["setup_v"], 1)
                n += 1
                ve.wait_ge(S["setup_v"], n)
            TS(upscale[:, :], wscale[:, 0:1], 0.5, None, ALU.mult)
            TT2(hidscale[:, :], wscale[:, 0:1], wscale[:, 1:2], ALU.mult).then_inc(S["setup_v"], 1)
            n += 1
            ve.wait_ge(S["setup_v"], n)
            STT(hidscale[:, :], hidscale[:, :], 0.5, wscale[:, 2:3], ALU.mult, ALU.mult)
            TS(wo[:, :, :], wo[:, :, :], nw[:, 0:1], 0.5, ALU.mult, ALU.mult)
            ve.wait_ge(S["a_exp"], 1)
            TS(smalls[:, :, C_A], smalls[:, :, C_A], -1.0, None, ALU.mult).then_inc(S["setup_ok"], 1)

            with ve.Fori(0, groups) as g:
                gu = Unit(ve, g)
                ve.wait_ge(S["x_in"], gu.dma)
                before(ve, gu, "mv_ok")
                for c in range(NC):
                    last = nc.vector.bn_stats(bst[:, c, :], xt[:, c, :])
                last.then_inc(S["bn_ok"], 1)
                constant_wait(ve)
                now(ve, gu, "bn_ok")
                before(ve, gu, "xn_ok")
                for c in range(NC):
                    last = nc.vector.bn_aggr(mv[:, c, :], bst[:, c, :])
                last.then_inc(S["mv_ok"], 1)
                now(ve, gu, "rstd_ok")
                before(ve, gu, "xT_mm")
                for c in range(NC):
                    last = TS(xn[:, c, :], xt[:, c, :], mv[:, c, 0:1], rstd[:, c:c + 1], ALU.subtract, ALU.mult)
                last.then_inc(S["xn_ok"], 1)
                now(ve, gu, "beta_exp")
                TS(beta[:, :, :], beta[:, :, :], 1.0, None, ALU.add).then_inc(S["beta_1"], 1)
                now(ve, gu, "beta_1")
                nc.vector.reciprocal(beta[:, :, :], beta[:, :, :]).then_inc(S["beta_ok"], 1)
                now(ve, gu, "beta_ok")
                project(Unit(ve, g * HEADS))
                with ve.Fori(0, HEADS - 1) as h:
                    attend(Unit(ve, g * HEADS + h), h)
                    project(Unit(ve, g * HEADS + h + 1))
                attend(Unit(ve, g * HEADS + HEADS - 1), HEADS - 1)
                for e in range(ET):
                    ve.wait_ge(S["ffn_tanh"], g * ET + e + 1)
                    STT(fu[:, :], ftan[:, :], 1.0, bQ[:, :], ALU.add, ALU.mult).then_inc(S["ffn_u"], 1)
                    ve.wait_ge(S["ffn_u"], g * ET + e + 1)
                    before(ve, gu, "group_mm")
                    STT(hid[:, e, :], fu[:, :], hidscale[:, 0:1], bK[:, :], ALU.mult, ALU.mult).then_inc(S["ffn_hid"], 1)
                now(ve, gu, "group_mm")
                for i in range(2):
                    last = TT2(ot[:, 2 * i:2 * i + 2, :], (bV, bG)[i][:, :].rearrange("p (c n) -> p c n", c=2),
                               xt[:, 2 * i:2 * i + 2, :], ALU.add)
                last.then_inc(S["out_ok"], 1)

        @block.gpsimd
        def _(gp):
            GT = nc.gpsimd.tensor_tensor
            prime(gp, "POOL")

            def small_cols(u, h):
                constant_wait(gp)
                before(gp, u, "cv3_k", "cv3_q", "cv3_v", "g_ready")
                nc.gpsimd.tensor_copy(sm[:, :], smalls[:, h, :]).then_inc(S["sm_ok"], 1)

            def up(u, h):
                if h == 1:
                    now(gp, u, "g_ready", "silu_k")
                    before(gp, u, "lv128_mm", "kq4", "kl4", "gg4")
                else:
                    now(gp, u, f"lv{h}_mm", f"gg{h}", f"kl{h}")
                    if h < 64:
                        before(gp, u, f"kq{4 * h}", f"kl{4 * h}")
                if h < 64:
                    g2 = halves(G[h][:, :], 1)
                    GT(G[2 * h][:, :].unsqueeze(2), g2[:, :, 0, :], g2[:, :, 1, :], ALU.mult)\
                        .then_inc(S[f"gg{2 * h}"], 1)
                    o = halves(KL[:, :], h)[:, :, 0, :]
                    s = halves(kq[:, 0, :], h)[:, :, 0, :] if h == 1 else o
                    g = g2[:, :, 1, :].to_broadcast([P, TOK // (2 * h), h])
                else:
                    o = KL[:, :].rearrange("p (b f t) -> p b f t", b=NB, f=4)[:, :, 0, :]
                    s = o
                    g = G[64][:, :].rearrange("p (b f) -> p b f", b=NB)[:, :, 1:2].to_broadcast([P, NB, 64])
                GT(o, s, g, ALU.mult).then_inc(S[f"kl{2 * h}"], 1)

            def norms(u):
                now(gp, u, "ssk_ok")
                before(gp, u, "v_norm")
                GT(nh[:, :], ssk4[:, :], const(K_HALF, NC), ALU.pow).then_inc(S["nh_ok"], 1)
                now(gp, u, "b2_ok")
                before(gp, u, "a2_ok", "a32_ok")
                GT(mb[:, :, :, :], const(K_SM, NSMALL * 16).rearrange("p (n s) -> p n s", s=16)
                   .unsqueeze(2).to_broadcast([P, NSMALL, NC, 16]),
                   b2n[:, :].unsqueeze(1).unsqueeze(3).to_broadcast([P, NSMALL, NC, 16]), ALU.mult)
                GT(mb32[:, :, :], const(K_M32, 2).unsqueeze(1).to_broadcast([P, NC, 2]),
                   b2n[:, :].unsqueeze(2).to_broadcast([P, NC, 2]), ALU.mult).then_inc(S["mb_ok"], 1)

            def scales(u):
                now(gp, u, "st_ok")
                before(gp, u, "rb_mm")
                GT(rr[:, :], st[:, :], const(K_NHALF, NC), ALU.pow).then_inc(S["rr_ok"], 1)

            def attend(u):
                up(u, 1)
                norms(u)
                for h in (2, 4, 8, 16, 32, 64):
                    up(u, h)
                scales(u)

            gp.wait_ge(S["setup_ok"], 1)
            with gp.Fori(0, groups) as g:
                gu = Unit(gp, g)
                constant_wait(gp)
                now(gp, gu, "mv_ok")
                before(gp, gu, "xn_ok")
                nc.gpsimd.tensor_scalar(rstd[:, :], mv[:, :, 1], LN_EPS, None, ALU.add).then_inc(S["rstd_e"], 1)
                gp.wait_ge(S["rstd_e"], g + 1)
                GT(rstd[:, :], rstd[:, :], const(K_NHALF, NC), ALU.pow).then_inc(S["rstd_ok"], 1)
                small_cols(Unit(gp, g * HEADS), 0)
                with gp.Fori(0, HEADS - 1) as h:
                    attend(Unit(gp, g * HEADS + h))
                    small_cols(Unit(gp, g * HEADS + h + 1), h + 1)
                attend(Unit(gp, g * HEADS + HEADS - 1))


def kernel(L0_attn_hidden_states, L0_attn_Wq, L0_attn_Wk, L0_attn_Wv, L0_attn_conv_q, L0_attn_conv_k,
           L0_attn_conv_v, L0_attn_A_log, L0_attn_Wfa, L0_attn_Wfb, L0_attn_dt_bias, L0_attn_Wb, L0_attn_Wga,
           L0_attn_Wgb, L0_attn_norm_w, L0_attn_Wo, L0_ffn_W_up, L0_ffn_W_gate, L0_ffn_W_down):
    import concourse.bacc as bacc
    from concourse.bass_utils import run_bass_kernel_spmd

    f = np.asarray
    x = f(L0_attn_hidden_states)
    groups = x.shape[0] // NB

    xg = x.reshape(groups, NC, P, HID).transpose(0, 2, 1, 3)

    def head_tiles(w):
        return f(w).reshape(-1, P, HEADS, P).transpose(2, 1, 0, 3)

    wh = np.concatenate([head_tiles(L0_attn_Wfb), head_tiles(L0_attn_Wk), head_tiles(L0_attn_Wq),
                         head_tiles(L0_attn_Wv)], axis=2).reshape(HEADS, P, WCOLS)
    wgb = head_tiles(L0_attn_Wgb).reshape(HEADS, P, P)
    small = np.zeros((P, HEADS, 16), np.float32)
    for c0, w in ((C_Q, L0_attn_conv_q), (C_K, L0_attn_conv_k), (C_V, L0_attn_conv_v)):
        small[:, :, c0:c0 + TAPS] = f(w).reshape(HEADS, P, TAPS).transpose(1, 0, 2)
    small[:, :, C_DT] = f(L0_attn_dt_bias).reshape(HEADS, P).T
    small[:, :, C_A] = np.broadcast_to(f(L0_attn_A_log).reshape(1, HEADS), (P, HEADS))

    def rows(w):
        return f(w).reshape(-1, P, w.shape[1]).transpose(1, 0, 2)

    arrays = {
        "x": xg, "wh": wh, "wgb": wgb, "small": small,
        "wfg": np.stack([rows(L0_attn_Wfa), rows(L0_attn_Wga)], axis=1),
        "wb": rows(L0_attn_Wb), "wo": rows(L0_attn_Wo), "nw": f(L0_attn_norm_w).reshape(P, 1),
        "wup": rows(f(L0_ffn_W_up).T), "wgt": rows(f(L0_ffn_W_gate).T), "wdn": rows(f(L0_ffn_W_down).T),
        "const": constants(),
    }
    arrays = {n: np.ascontiguousarray(a) for n, a in arrays.items()}
    nc = bacc.Bacc("TRN2", target_bir_lowering=False, num_devices=1)
    args = [nc.dram_tensor(f"{n}_dram", a.shape, F32, kind="ExternalInput").ap() for n, a in arrays.items()]
    out = nc.dram_tensor("out_dram", (groups, P, NC, HID), F32, kind="ExternalOutput").ap()
    build(nc, *args, out)
    r = run_bass_kernel_spmd(nc, [{f"{n}_dram": a for n, a in arrays.items()}], core_ids=[0])
    y = np.asarray(r.results[0]["out_dram"])
    return y.transpose(0, 2, 1, 3).reshape(x.shape)
```

```python
from contextlib import ExitStack

import numpy as np

import concourse.bass as bass
from concourse import mybir

F32 = mybir.dt.float32
U32 = mybir.dt.uint32
ALU = mybir.AluOpType
ACT = mybir.ActivationFunctionType
AX = mybir.AxisListType

P = 128
NB = 2
T = 256
TOK = NB * T
NC = TOK // P
HEADS = 16
HID = 256
KT = HID // P
EXP = 1024
ET = EXP // P
SB = 32
H = P // 2
TAPS = 4
LEVELS = (1, 2, 4, 8, 16, 32)
NLEV = len(LEVELS)

W_F, W_K, W_Q, W_V = 0, 1, 3, 5
WCOLS = 7 * P
C_Q, C_K, C_V, C_DT, C_A, C_N = 0, 4, 8, 12, 13, 14

K_ID = 0
K_ID64 = K_ID + P
K_SM = K_ID64 + H
K_OSC = K_SM + NLEV * SB
K_QSC = K_OSC + H
K_HALF = K_QSC + H
K_NHALF = K_HALF + NC
K_ONES = K_NHALF + NC
K_COLS = K_ONES + P

LN_EPS = 1e-5
QK_EPS = 4e-6
O_EPS = 1e-6


def constants():
    c = np.zeros((P, K_COLS), np.float32)
    i = np.arange(P)
    c[i, K_ID + i] = 1
    c[i, K_ID64 + i % H] = 1
    for n, h in enumerate(LEVELS):
        for j in range(SB):
            t = (j // h) * 2 * h + h + j % h
            c[:, K_SM + SB * n + j] = (i % H // (2 * h) == t // (2 * h)) & (i % (2 * h) < h)
    c[:, K_OSC:K_OSC + H] = 1.0 / P
    c[:, K_QSC:K_QSC + H] = P * O_EPS
    c[:, K_HALF:K_HALF + NC] = 0.5
    c[:, K_NHALF:K_NHALF + NC] = -0.5
    c[:, K_ONES:K_ONES + P] = 1.0
    return c


def build(nc, x_d, wh_d, wgb_d, sm_d, wfg_d, wb_d, wo_d, nw_d, wup_d, wgt_d, wdn_d, const_d, out_d):
    groups = x_d.shape[0]
    ctx = ExitStack()
    with ctx:
        def sb(name, shape, dt=F32):
            return ctx.enter_context(nc.sbuf_tensor(name, shape, dt))

        def bank(name):
            return ctx.enter_context(nc.psum_tensor(name, [P, 512], F32))

        cst = sb("cst", [P, K_COLS])
        smalls = sb("smalls", [P, HEADS, 16])
        wfg = sb("wfg", [P, 2, KT, P])
        wb = sb("wb", [P, KT, HEADS])
        wo = sb("wo", [P, HEADS, HID])
        nw = sb("nw", [P, 1])
        wup = sb("wup", [P, KT, EXP])
        wgt = sb("wgt", [P, KT, EXP])
        wdn = sb("wdn", [P, ET, HID])
        wsum = sb("wsum", [P, 3])
        wscale = sb("wscale", [P, 3])
        wthr = sb("wthr", [P, 6])
        upscale = sb("upscale", [P, 1])
        hidscale = sb("hidscale", [P, 1])
        xt = sb("xt", [P, NC, HID])
        xn = sb("xn", [P, NC, HID])
        bst = sb("bst", [P, NC, 6])
        mv = sb("mv", [P, NC, 2])
        rstd = sb("rstd", [P, NC])
        xnT = sb("xnT", [P, KT, TOK])
        faT = sb("faT", [P, TOK])
        gaT = sb("gaT", [P, TOK])
        beta = sb("beta", [P, HEADS, NC])
        OG = sb("OG", [P, HEADS, TOK])
        tern = OG[:, 0:4, :].rearrange("p a b -> p (a b)")
        tern2 = OG[:, 4:8, :].rearrange("p a b -> p (a b)")
        work = sb("work", [P, ET, TOK])
        acc, th, kq, hid = work[:, 0:3, :], work[:, 3:6, :], work[:, 6:8, :], work
        ftan = sb("ftan", [P, TOK])
        fu = sb("fu", [P, TOK])
        xres = sb("xres", [P, NC, HID])
        ot = sb("ot", [P, NC, HID])
        wh = [sb(f"wh{p}", [P, WCOLS]) for p in range(2)]
        wgb = sb("wgb", [P, P])
        sm = sb("sm", [P, 16])
        gbuf = sb("gbuf", [P, TOK])
        vv = sb("vv", [P, TOK])
        G = {1 << n: sb(f"G{1 << n}", [P, TOK >> n]) for n in range(7)}
        KQ = sb("KQ", [P, 2, TOK])
        KL = sb("KL", [P, TOK])
        ksq = sb("ksq", [P, TOK])
        ssk = sb("ssk", [P, NC])
        ssk4 = sb("ssk4", [P, NC])
        rec = sb("rec", [P, NC])
        b2n = sb("b2n", [P, NC])
        nh = sb("nh", [P, NC])
        mb = sb("mb", [P, NLEV, NC, SB])
        qsq = [sb(f"qsq{p}", [P, TOK]) for p in range(2)]
        b2 = [sb(f"b2_{p}", [P, NC]) for p in range(2)]
        L = [sb(f"L{p}", [P, NLEV, NC, H]) for p in range(2)]
        LT64 = [sb(f"LT64_{p}", [P, NC, 64]) for p in range(2)]
        AQ = [sb(f"AQ{p}", [P, NC, P]) for p in range(2)]
        AXc = [sb(f"AX{p}", [P, NB, 2 * P]) for p in range(2)]
        Vn = [sb(f"Vn{p}", [P, NC, P]) for p in range(2)]
        Tm = sb("Tm", [P, NC, H])
        Tt = sb("Tt", [P, NC, H])
        M = sb("M", [P, NC, H])
        Tx = sb("Tx", [P, NC, P])
        M64 = sb("M64", [P, NC, 64])
        R = sb("R", [P, NB, P])
        U = sb("U", [P, NC, P])
        sg = sb("sg", [P, TOK])
        OGr = sb("OGr", [P, TOK])
        osq = sb("osq", [P, TOK])
        st = sb("st", [P, NC])
        rr = sb("rr", [P, NC])

        bX, bY, bG, bA, bB, bT, bS, bM = [bank(f"bank{i}") for i in range(8)]
        bconv = [bX, bY, bX]
        ffn_banks = ((bX, bY), (bG, bA))
        level_bank = {1: bB, 2: bA, 4: bB, 8: bA, 16: bB, 32: bA}

        S = {}

        PER_HEAD = {
            "PE": ["proj_g", "proj_k", "proj_q", "proj_v", "ssk_mm", "diag_mm", "vT_mm",
                   "lv1_mm", "lv2_mm", "lv4_mm", "lv8_mm", "lv16_mm", "lv32_mm", "lv64_mm", "lv128_mm",
                   "t1_mm", "m2_mm", "m4_mm", "m8_mm", "m16_mm", "t2_mm", "t4_mm", "t8_mm", "t16_mm",
                   "m32_mm", "t32_mm", "m64_mm", "t64_mm", "u0_mm", "x_mm", "u1_mm", "o_mm", "st_mm",
                   "rb_mm", "gg_mm"],
            "ACT": ["tap_k", "tap_q", "tap_v", "g_exp", "g_ln", "g_ready", "tanh_k", "tanh_q", "tanh_v",
                    "ksq_ok", "qsq_ok", "kl_odd", "v_norm", "q64_ok", "ax_ok",
                    "m2_ok", "m4_ok", "m8_ok", "m16_ok", "m32_ok", "m64_ok", "t64_ok", "u0_ok", "u1_ok", "osq_ok", "sg_ok"],
            "DVE": ["g_min", "g_max"] + [f"cv{j}_{n}" for j in (1, 2, 3) for n in "kqv"]
                   + ["silu_k", "silu_q", "silu_v", "ssk_ok", "rec_ok", "b2_ok", "kq1", "kq2", "kq4", "kq8",
                      "kq16", "kq32", "kq64", "kq128", "ev0", "ev1", "ev2", "ev4", "ev8", "ev16", "ev32",
                      "k64_ok", "tt1", "t1_ok", "t2_ok", "t4_ok", "t8_ok", "t16_ok", "t32_ok", "s2_ok", "s4_ok", "s8_ok", "s16_ok", "s32_ok", "r_ok", "og_raw", "st_ok",
                      "og_ok"],
            "POOL": ["sm_ok", "kl2", "kl4", "kl8", "kl16", "kl32", "kl64", "kl128", "nh_ok",
                     "mb0", "mb1", "mb2", "rr_ok"],
        }
        PER_GROUP = {
            "PE": ["xT_mm", "fg_mm", "beta_mm", "group_mm"],
            "ACT": ["xT_ok", "fa_ok", "ga_ok", "beta_exp"],
            "DVE": ["bn_ok", "mv_ok", "xn_ok", "beta_1", "beta_ok", "out_ok"],
            "POOL": ["rstd_ok"],
        }

        ONCE = ["const_in", "x_in", "w_in0", "w_in1", "wgb_in", "out_done", "wsum_ok", "wsum_mm", "zero_ok", "setup_v",
                "setup_ok", "a_exp", "rstd_e", "ffn_mm", "ffn_tanh", "ffn_u", "ffn_hid"]
        for names in (*PER_HEAD.values(), *PER_GROUP.values(), ONCE):
            for name in names:
                S[name] = ctx.enter_context(nc.semaphore(name))

        def prime(eng, who):
            for name in PER_HEAD[who] + PER_GROUP[who]:
                eng.sem_inc(S[name], 2)

        class Unit:
            def __init__(self, eng, n, h=None, odd=0):
                self.n, self.h = n, h
                self.w = n * 8 + 16 - 8 * odd
                self.now, self.before, self.older, self.dma = n + 3, n + 2, n + 1, n * 16 + 16
                if not isinstance(n, int):
                    self.now, self.before, self.older = (eng.snap(v) for v in (self.now, self.before, self.older))
                    for v in (self.now, self.before, self.older):
                        eng.compute_val(v)
                    if eng in (nc.sync, nc.tensor):
                        self.dma = eng.snap(self.dma)
                        eng.compute_val(self.dma)
                    if eng is nc.tensor:
                        self.w = eng.snap(self.w)
                        eng.compute_val(self.w)

        def now(eng, u, *names):
            for n in names:
                eng.wait_ge(S[n], u.now)

        def before(eng, u, *names):
            for n in names:
                eng.wait_ge(S[n], u.before)

        def older(eng, u, *names):
            for n in names:
                eng.wait_ge(S[n], u.older)

        def pipeline(eng, g, step, last):
            def units(h0, n):
                return [Unit(eng, g * HEADS + h0 + i, h0 + i, i % 2) for i in range(n)]

            u = units(0, 3)
            step(u[0], None, u[1], None, 0)
            step(u[1], u[0], u[2], None, 1)
            with eng.Fori(0, HEADS // 2 - 2) as i:
                v = units(2 * i, 5)
                step(v[2], v[1], v[3], v[0], 0)
                step(v[3], v[2], v[4], v[1], 1)
            u = units(HEADS - 4, 4)
            step(u[2], u[1], u[3], u[0], 0)
            step(u[3], u[2], None, u[1], 1)
            last(u[3], u[2])

        def constant_wait(eng):
            eng.wait_ge(S["setup_ok"], 1)

        def halves(ap, h):
            d = " ".join(f"a{i}" for i in range(len(ap.shape) - 1))
            return ap.rearrange(f"{d} (n two h) -> {d} n two h", two=2, h=h)

        def chunk_halves():
            return [(c, c * P + s * H, slice(s * H, (s + 1) * H)) for c in range(NC) for s in range(2)]

        def const(c0, n):
            return cst[:, c0:c0 + n]

        block = ctx.enter_context(nc.Block())

        @block.sync
        def _(sp):
            sp.sem_inc(S["out_done"], 16)
            for dst, src in ((cst[:, :], const_d), (wup[:, :, :], wup_d), (wgt[:, :, :], wgt_d),
                             (wdn[:, :, :], wdn_d), (smalls[:, :, :], sm_d), (wfg[:, :, :, :], wfg_d),
                             (wb[:, :, :], wb_d), (wo[:, :, :], wo_d), (nw[:, :], nw_d)):
                sp.dma_start(dst, src).then_inc(S["const_in"], 16)

            def load_x(g, gu):
                before(sp, gu, "beta_exp")
                sp.dma_start(xt[:, :, :], x_d[g]).then_inc(S["x_in"], 16)

            def load_w(u, h, p):
                older(sp, u, "proj_v")
                sp.dma_start(wh[p][:, :], wh_d[h]).then_inc(S[f"w_in{p}"], 16)

            def load_wgb(u, h):
                before(sp, u, "gg_mm")
                sp.dma_start(wgb[:, :], wgb_d[h]).then_inc(S["wgb_in"], 16)

            def group(g, more):
                gu = Unit(sp, g)
                for p in range(2):
                    load_w(Unit(sp, g * HEADS + p), p, p)
                if more:
                    load_x(g + 1, Unit(sp, g + 1))
                with sp.Fori(0, HEADS // 2 - 1) as i:
                    for p in range(2):
                        h = 2 * i + p
                        load_wgb(Unit(sp, g * HEADS + h), h)
                        load_w(Unit(sp, g * HEADS + h + 2), h + 2, p)
                for h in (HEADS - 2, HEADS - 1):
                    load_wgb(Unit(sp, g * HEADS + h), h)
                now(sp, gu, "out_ok")
                sp.dma_start(out_d[g], ot[:, :, :]).then_inc(S["out_done"], 16)

            load_x(0, Unit(sp, 0))
            if groups > 1:
                with sp.Fori(0, groups - 1) as g:
                    group(g, True)
            group(groups - 1, False)
            sp.wait_ge(S["out_done"], 16 * groups + 16)

        @block.tensor
        def _(pe):
            mm = nc.tensor.matmul
            prime(pe, "PE")

            def proj_g(u, b, p):
                pe.wait_ge(S[f"w_in{p}"], u.w)
                before(pe, u, "g_max")
                if b:
                    now(pe, b, "v_norm")
                mm(bG[:, :], wh[p][:, W_F * P:(W_F + 1) * P], faT[:, :], start=True, stop=True)\
                    .then_inc(S["proj_g"], 1)

            def proj(u, n, t, p):
                bnk, w0 = {"k": (bX, W_K), "q": (bY, W_Q), "v": (bX, W_V)}[n]
                if t == 0:
                    if n == "v":
                        now(pe, u, "cv3_k")
                    else:
                        before(pe, u, {"k": "cv3_v", "q": "cv3_q"}[n])
                last = mm(bnk[:, :], wh[p][:, (w0 + t) * P:(w0 + t + 1) * P], xnT[:, t, :],
                          start=(t == 0), stop=(t == KT - 1))
                if t == KT - 1:
                    last.then_inc(S[f"proj_{n}"], 1)

            def key_norms(u):
                now(pe, u, "ksq_ok")
                for c in range(NC):
                    last = mm(bM[:, c * H:(c + 1) * H], ksq[:, c * P:(c + 1) * P], const(K_ONES, H), start=True, stop=True)
                last.then_inc(S["ssk_mm"], 1)

            def diagonal(u):
                now(pe, u, "silu_k", "silu_q")
                before(pe, u, "ax_ok")
                for c in range(NC):
                    last = mm(bA[:, c * P:(c + 1) * P], kq[:, 0, c * P:(c + 1) * P], kq[:, 1, c * P:(c + 1) * P],
                              start=True, stop=True)
                last.then_inc(S["diag_mm"], 1)

            def v_turn(u, b, c):
                now(pe, u, "silu_v")
                if b:
                    now(pe, b, "sg_ok")
                else:
                    now(pe, c, "g_max")
                for k in range(NC):
                    last = nc.tensor.transpose(bG[:, k * P:(k + 1) * P], vv[:, k * P:(k + 1) * P], const(K_ID, P))
                last.then_inc(S["vT_mm"], 1)

            def level(u, h):
                bnk = level_bank[h]
                left = kq[:, 0, :] if h == 1 else KL[:, :]
                constant_wait(pe)
                now(pe, u, f"kq{h}")
                if h > 1:
                    now(pe, u, f"kl{h}", f"ev{h // 4}")
                else:
                    before(pe, u, "q64_ok", "k64_ok")
                if h == 2:
                    now(pe, u, "kl_odd")
                for c, t0, rows in chunk_halves():
                    right = halves(KQ[:, :, t0:t0 + H], h)[:, :, :, 1, :]
                    last = mm(bnk[rows, c * H:(c + 1) * H].rearrange("p (k n h) -> p k n h", k=2, h=h),
                              left[:, t0:t0 + H], right, start=True, stop=True)
                last.then_inc(S[f"lv{h}_mm"], 1)

            def level64(u):
                now(pe, u, "kq64", "kl64", "ev16")
                for c in range(NC):
                    last = mm(bB[0:64, c * P:(c + 1) * P].rearrange("p (k h) -> p k h", k=2),
                              KL[:, c * P:c * P + 64], KQ[:, :, c * P + 64:(c + 1) * P], start=True, stop=True)
                last.then_inc(S["lv64_mm"], 1)

            def level128(u):
                now(pe, u, "kq128", "kl128", "ev32")
                for b in range(NB):
                    last = mm(bA[:, b * T:(b + 1) * T].rearrange("p (k h) -> p k h", k=2),
                              KL[:, b * T:b * T + P], KQ[:, :, b * T + P:(b + 1) * T], start=True, stop=True)
                last.then_inc(S["lv128_mm"], 1)

            def inv_first(u, p):
                constant_wait(pe)
                now(pe, u, "ev1")
                for c, _, rows in chunk_halves():
                    last = mm(bM[rows, NC * H + c * H:NC * H + (c + 1) * H], L[p][rows, 0, c, :], cst[rows, K_ID64:K_ID64 + H],
                              start=True, stop=True)
                last.then_inc(S["t1_mm"], 1)

            def inv_m(u, p, h, a=None):
                constant_wait(pe)
                now(pe, u, f"ev{h}", f"t{h // 2}_ok")
                if h == 2 and a:
                    now(pe, a, "ssk_ok")
                for c, _, rows in chunk_halves():
                    last = mm(bM[rows, c * H:(c + 1) * H], L[p][rows, LEVELS.index(h), c, :], Tm[rows, c, :],
                              start=True, stop=True)
                last.then_inc(S[f"m{h}_mm"], 1)

            def inv_t(u, h):
                constant_wait(pe)
                now(pe, u, f"m{h}_ok", f"s{h // 2}_ok" if h > 2 else "tt1")
                if h == 2:
                    before(pe, u, "og_ok")
                for c, _, rows in chunk_halves():
                    mm(bT[rows, c * H:(c + 1) * H], Tt[rows, c, :], M[rows, c, :], start=True, stop=True)
                    last = mm(bS[rows, c * H:(c + 1) * H], M[rows, c, :], Tt[rows, c, :], start=True, stop=True)
                last.then_inc(S[f"t{h}_mm"], 1)

            def inv_m64(u, p):
                constant_wait(pe)
                now(pe, u, "k64_ok", "t32_ok")
                for c in range(NC):
                    last = mm(bM[64:128, c * 64:(c + 1) * 64], LT64[p][0:64, c, :], Tm[0:64, c, :],
                              start=True, stop=True)
                last.then_inc(S["m64_mm"], 1)

            def inv_t64(u):
                constant_wait(pe)
                now(pe, u, "m64_ok", "s32_ok")
                for c in range(NC):
                    last = mm(bM[0:64, 256 + c * 64:256 + (c + 1) * 64], M64[64:128, c, :], Tt[64:128, c, :],
                              start=True, stop=True)
                last.then_inc(S["t64_mm"], 1)

            def solve_0(u, p):
                now(pe, u, "t64_ok", "v_norm")
                for b in range(NB):
                    last = mm(bM[:, b * P:(b + 1) * P], Tx[:, 2 * b, :], Vn[p][:, 2 * b, :], start=True, stop=True)
                last.then_inc(S["u0_mm"], 1)

            def solve_x(u, p):
                now(pe, u, "u0_ok", "ax_ok")
                for b in range(NB):
                    last = mm(bM[:, (2 + b) * P:(3 + b) * P], AXc[p][:, b, 0:P], U[:, 2 * b, :],
                              start=True, stop=True)
                last.then_inc(S["x_mm"], 1)

            def solve_1(u):
                now(pe, u, "r_ok")
                for b in range(NB):
                    last = mm(bM[:, b * P:(b + 1) * P], Tx[:, 2 * b + 1, :], R[:, b, :], start=True, stop=True)
                last.then_inc(S["u1_mm"], 1)

            def output(u, p):
                now(pe, u, "u1_ok", "q64_ok", "ev32")
                for b in range(NB):
                    c0, c1 = 2 * b, 2 * b + 1
                    mm(bS[:, c0 * P:(c0 + 1) * P], U[:, c0, :], AQ[p][:, c0, :], start=True, stop=True)
                    mm(bS[:, c1 * P:(c1 + 1) * P], U[:, c0, :], AXc[p][:, b, P:2 * P], start=True, stop=False)
                    last = mm(bS[:, c1 * P:(c1 + 1) * P], U[:, c1, :], AQ[p][:, c1, :], start=False, stop=True)
                last.then_inc(S["o_mm"], 1)

            def gate2(u, c):
                pe.wait_ge(S["wgb_in"], u.dma)
                if c:
                    now(pe, c, "g_max")
                else:
                    now(pe, u, "v_norm")
                mm(bG[:, :], wgb[:, :], gaT[:, :], start=True, stop=True).then_inc(S["gg_mm"], 1)

            def out_norms(u, p):
                now(pe, u, "osq_ok", "t32_ok", "qsq_ok")
                for c in range(NC):
                    mm(bT[:, c * H:(c + 1) * H], osq[:, c * P:(c + 1) * P], const(K_OSC, H), start=True, stop=False)
                    last = mm(bT[:, c * H:(c + 1) * H], qsq[p][:, c * P:(c + 1) * P], const(K_QSC, H),
                              start=False, stop=True)
                last.then_inc(S["st_mm"], 1)

            def spread(u):
                now(pe, u, "rr_ok")
                for c in range(NC):
                    last = mm(bT[:, c * P:(c + 1) * P], rr[:, c:c + 1].to_broadcast([P, P]), const(K_ID, P),
                              start=True, stop=True)
                last.then_inc(S["rb_mm"], 1)

            def step(a, b, c, d, p):
                if c:
                    proj_g(c, b, 1 - p)
                fill = {2: ("k0", "k1"), 4: ("q0", "q1"), 8: ("", "v0"), 16: ("", "g"), 32: ("", "v1")}

                def dense(what):
                    if what == "g":
                        if b:
                            gate2(b, c)
                    elif what and c:
                        proj(c, what[0], int(what[1]), 1 - p)

                for h in LEVELS[1:]:
                    if b:
                        inv_m(b, 1 - p, h, a)
                    if d and h == 2:
                        spread(d)
                    if a:
                        level(a, h)
                    dense(fill[h][0])
                    if b:
                        inv_t(b, h)
                    dense(fill[h][1])
                if b:
                    inv_m64(b, 1 - p)
                if a:
                    level64(a)
                if b:
                    inv_t64(b)
                if a:
                    level128(a)
                if b:
                    solve_0(b, 1 - p)
                if a:
                    v_turn(a, b, c)
                if b:
                    solve_x(b, 1 - p)
                if c:
                    diagonal(c)
                if b:
                    solve_1(b)
                if c:
                    level(c, 1)
                if b:
                    output(b, 1 - p)
                if a:
                    inv_first(a, p)
                if c:
                    key_norms(c)
                if b:
                    out_norms(b, 1 - p)

            def group_in(gu):
                now(pe, gu, "xn_ok")
                before(pe, gu, "out_ok")
                for c in range(NC):
                    for t in range(KT):
                        last = nc.tensor.transpose((bX, bY)[t][:, c * P:(c + 1) * P], xn[:, c, t * P:(t + 1) * P],
                                                   const(K_ID, P))
                last.then_inc(S["xT_mm"], 1)
                now(pe, gu, "xT_ok")
                for i, bnk in enumerate((bT, bS)):
                    for t in range(KT):
                        last = mm(bnk[:, :], wfg[:, i, t, :], xnT[:, t, :], start=(t == 0), stop=(t == KT - 1))
                last.then_inc(S["fg_mm"], 1)
                for c in range(NC):
                    for t in range(KT):
                        last = mm(bA[:, c * HEADS:(c + 1) * HEADS], xnT[:, t, c * P:(c + 1) * P], wb[:, t, :],
                                  start=(t == 0), stop=(t == KT - 1))
                last.then_inc(S["beta_mm"], 1)
                now(pe, gu, "fa_ok", "ga_ok", "beta_exp")

            def expert(g, e, b):
                if e == 0:
                    now(pe, b, "cv3_k", "cv3_q", "cv3_v")
                if e == 1:
                    now(pe, b, "sg_ok", "ax_ok")
                if e >= 2:
                    pe.wait_ge(S["ffn_hid"], g * ET + e - 1)
                for bnk, w in zip(ffn_banks[e % 2], (wup, wgt)):
                    for t in range(KT):
                        last = mm(bnk[:, :], w[:, t, e * P:(e + 1) * P], xnT[:, t, :],
                                  start=(t == 0), stop=(t == KT - 1))
                last.then_inc(S["ffn_mm"], 1)

            def last_head(g, b, d):
                gate2(b, None)
                spread(d)
                expert(g, 0, b)
                for e, h in enumerate(LEVELS[1:]):
                    inv_m(b, 1, h)
                    expert(g, e + 1, b)
                    inv_t(b, h)
                inv_m64(b, 1)
                expert(g, 6, b)
                inv_t64(b)
                solve_0(b, 1)
                expert(g, 7, b)
                solve_x(b, 1)
                solve_1(b)
                output(b, 1)
                out_norms(b, 1)
                spread(b)

            def group_out(g, gu):
                pe.wait_ge(S["ffn_hid"], g * ET + ET)
                now(pe, Unit(pe, g * HEADS + HEADS - 1), "og_ok")
                for c in range(NC):
                    o = (bT, bS)[c // 2][:, (c % 2) * HID:(c % 2 + 1) * HID]
                    for h in range(HEADS):
                        mm(o, OG[:, h, c * P:(c + 1) * P], wo[:, h, :], start=(h == 0), stop=False)
                    for e in range(ET):
                        last = mm(o, hid[:, e, c * P:(c + 1) * P], wdn[:, e, :], start=False, stop=(e == ET - 1))
                last.then_inc(S["group_mm"], 1)

            pe.wait_ge(S["const_in"], 16 * 9)
            pe.wait_ge(S["wsum_ok"], 3)
            mm(bX[:, 0:3], const(K_ONES, P), wsum[:, :], start=True, stop=True).then_inc(S["wsum_mm"], 1)
            pe.wait_ge(S["setup_ok"], 1)
            with pe.Fori(0, groups) as g:
                gu = Unit(pe, g)
                group_in(gu)
                first = Unit(pe, g * HEADS)
                proj_g(first, None, 0)
                for n in "kqv":
                    for t in range(KT):
                        proj(first, n, t, 0)
                key_norms(first)
                diagonal(first)
                level(first, 1)
                pipeline(pe, g, step, lambda b, d: last_head(g, b, d))
                group_out(g, gu)

        @block.scalar
        def _(act):
            A = nc.scalar.activation
            prime(act, "ACT")

            def tap(u, n):
                i, c0 = {"k": (0, C_K), "q": (1, C_Q), "v": (2, C_V)}[n]
                now(act, u, "sm_ok", f"proj_{n}")
                before(act, u, f"silu_{n}")
                A(acc[:, i, :], bconv[i][:, :], ACT.Copy, scale=sm[:, c0 + 3:c0 + 4]).then_inc(S[f"tap_{n}"], 1)

            def gate_exp(u):
                now(act, u, "g_min")
                A(gbuf[:, :], gbuf[:, :], ACT.Exp).then_inc(S["g_exp"], 1)

            def gate_ln(u):
                now(act, u, "g_exp")
                A(gbuf[:, :], gbuf[:, :], ACT.Ln, bias=1.0).then_inc(S["g_ln"], 1)

            def gate_out(u):
                now(act, u, "g_max")
                before(act, u, "kq1", "kq2", "kl2")
                A(G[1][:, :], gbuf[:, :], ACT.Exp, scale=sm[:, C_A:C_A + 1]).then_inc(S["g_ready"], 1)

            def tanh(u, n):
                i = "kqv".index(n)
                now(act, u, f"cv3_{n}")
                before(act, u, f"silu_{n}")
                A(th[:, i, :], acc[:, i, :], ACT.Tanh, scale=0.5).then_inc(S[f"tanh_{n}"], 1)

            def key_copies(u):
                now(act, u, "silu_k")
                before(act, u, "ssk_mm")
                A(ksq[:, :], kq[:, 0, :], ACT.Square).then_inc(S["ksq_ok"], 1)
                before(act, u, "lv128_mm")
                A(halves(KL[:, :], 1)[:, :, 1, :], halves(kq[:, 0, :], 1)[:, :, 1, :], ACT.Copy)\
                    .then_inc(S["kl_odd"], 1)

            def query_squares(u, p):
                now(act, u, "silu_q")
                older(act, u, "st_mm")
                A(qsq[p][:, :], kq[:, 1, :], ACT.Square).then_inc(S["qsq_ok"], 1)

            def v_norm(u, p):
                now(act, u, "nh_ok", "vT_mm")
                older(act, u, "u0_mm", "r_ok")
                for c in range(NC):
                    last = A(Vn[p][:, c, :], bG[:, c * P:(c + 1) * P], ACT.Copy, scale=nh[:, c:c + 1])
                last.then_inc(S["v_norm"], 1)

            def inv_m(u, h):
                now(act, u, f"m{h}_mm")
                A(M[:, :, :], bM[:, 0:NC * H].rearrange("p (c s) -> p c s", c=NC), ACT.Copy).then_inc(S[f"m{h}_ok"], 1)

            def whole_chunks(u):
                now(act, u, "s32_ok")
                before(act, u, "u1_mm")
                for r in (slice(0, H), slice(H, P)):
                    A(Tx[r, :, r], Tt[r, :, :], ACT.Copy)

            def inv_m64(u):
                now(act, u, "m64_mm")
                A(M64[64:128, :, :], bM[64:128, 0:256].rearrange("p (c s) -> p c s", c=NC), ACT.Copy)\
                    .then_inc(S["m64_ok"], 1)

            def inv_t64(u):
                now(act, u, "t64_mm")
                A(Tx[0:64, :, 64:128], bM[0:64, 256:512].rearrange("p (c s) -> p c s", c=NC), ACT.Copy)\
                    .then_inc(S["t64_ok"], 1)

            def level64(u, p):
                now(act, u, "k64_ok")
                older(act, u, "o_mm")
                A(AQ[p][0:64, :, 64:128],
                  bB[0:64, :].rearrange("p (c k s) -> p c k s", c=NC, k=2)[:, :, 1, :], ACT.Copy)\
                    .then_inc(S["q64_ok"], 1)

            def level128(u, p):
                now(act, u, "lv128_mm")
                older(act, u, "o_mm")
                A(AXc[p][:, :, :], bA[:, :].rearrange("p (b s) -> p b s", b=NB), ACT.Copy).then_inc(S["ax_ok"], 1)

            def solve(u, p, part):
                now(act, u, f"u{part}_mm")
                if part == 0:
                    before(act, u, "o_mm")
                for b in range(NB):
                    c = 2 * b + part
                    last = A(U[:, c, :], bM[:, b * P:(b + 1) * P], ACT.Copy, scale=b2[p][:, c:c + 1])
                last.then_inc(S[f"u{part}_ok"], 1)

            def gate2(u):
                now(act, u, "gg_mm")
                before(act, u, "og_raw")
                A(sg[:, :], bG[:, :], ACT.Tanh, scale=0.5).then_inc(S["sg_ok"], 1)

            def out_sq(u):
                now(act, u, "o_mm")
                before(act, u, "st_mm")
                A(osq[:, :], bS[:, :], ACT.Square).then_inc(S["osq_ok"], 1)

            def step(a, b, c, d, p):
                if a:
                    query_squares(a, p)
                if b:
                    inv_m(b, 2)
                if c:
                    gate_exp(c)
                if a:
                    tanh(a, "v")
                if c:
                    tap(c, "k")
                if b:
                    inv_m(b, 4)
                if c:
                    gate_ln(c)
                    tap(c, "q")
                if b:
                    inv_m(b, 8)
                if c:
                    gate_out(c)
                if b:
                    inv_m(b, 16)
                if c:
                    tanh(c, "k")
                if b:
                    gate2(b)
                    inv_m(b, 32)
                if c:
                    tanh(c, "q")
                    tap(c, "v")
                if b:
                    inv_m64(b)
                    whole_chunks(b)
                if b:
                    inv_t64(b)
                if a:
                    level64(a, p)
                if b:
                    solve(b, 1 - p, 0)
                if a:
                    level128(a, p)
                if c:
                    key_copies(c)
                if b:
                    solve(b, 1 - p, 1)
                    out_sq(b)
                if a:
                    v_norm(a, p)

            def expert(g, e):
                act.wait_ge(S["ffn_mm"], g * ET + e + 1)
                if e:
                    act.wait_ge(S["ffn_hid"], g * ET + e)
                A(ftan[:, :], ffn_banks[e % 2][0][:, :], ACT.Tanh, scale=upscale[:, 0:1]).then_inc(S["ffn_tanh"], 1)

            def last_head(g, b, d):
                gate2(b)
                expert(g, 0)
                for e, h in enumerate(LEVELS[1:]):
                    inv_m(b, h)
                    expert(g, e + 1)
                inv_m64(b)
                whole_chunks(b)
                expert(g, 6)
                inv_t64(b)
                solve(b, 1, 0)
                expert(g, 7)
                solve(b, 1, 1)
                out_sq(b)

            act.wait_ge(S["const_in"], 16 * 9)
            for i, w in enumerate((wup, wgt, wdn)):
                if i:
                    act.wait_ge(S["wsum_ok"], i)
                A(tern[:, :], w[:, :, :].rearrange("p a b -> p (a b)"), ACT.Abs,
                  accum_out=wsum[:, i:i + 1]).then_inc(S["wsum_ok"], 1)
            A(smalls[:, :, C_A], smalls[:, :, C_A], ACT.Exp).then_inc(S["a_exp"], 1)

            act.wait_ge(S["setup_ok"], 1)
            with act.Fori(0, groups) as g:
                gu = Unit(act, g)
                now(act, gu, "xT_mm")
                for t in range(KT):
                    last = A(xnT[:, t, :], (bX, bY)[t][:, :], ACT.Copy)
                last.then_inc(S["xT_ok"], 1)
                before(act, gu, "out_ok")
                A(xres[:, :, :], xt[:, :, :], ACT.Copy)
                now(act, gu, "fg_mm")
                A(faT[:, :], bT[:, :], ACT.Copy).then_inc(S["fa_ok"], 1)
                A(gaT[:, :], bS[:, :], ACT.Copy).then_inc(S["ga_ok"], 1)
                now(act, gu, "beta_mm")
                first = Unit(act, g * HEADS)
                before(act, first, "b2_ok")
                A(beta[:, :, :].rearrange("p h c -> p c h"), bA[:, 0:HEADS * NC].rearrange("p (c h) -> p c h", c=NC),
                  ACT.Exp, scale=-1.0).then_inc(S["beta_exp"], 1)
                gate_exp(first)
                gate_ln(first)
                gate_out(first)
                for n in "kqv":
                    tap(first, n)
                for n in "kq":
                    tanh(first, n)
                key_copies(first)
                pipeline(act, g, step, lambda b, d: last_head(g, b, d))

        @block.vector
        def _(ve):
            TT2 = nc.vector.tensor_tensor
            TS = nc.vector.tensor_scalar
            STT = nc.vector.scalar_tensor_tensor
            prime(ve, "DVE")

            def gate_min(u):
                now(ve, u, "sm_ok", "proj_g")
                before(ve, u, "g_ready")
                TS(gbuf[:, :], bG[:, :], sm[:, C_DT:C_DT + 1], 40.0, ALU.add, ALU.min).then_inc(S["g_min"], 1)

            def gate_max(u):
                now(ve, u, "g_ln")
                STT(gbuf[:, :], bG[:, :], sm[:, C_DT:C_DT + 1], gbuf[:, :], ALU.add, ALU.max).then_inc(S["g_max"], 1)

            def conv(u, n, j):
                i, c0 = {"k": (0, C_K), "q": (1, C_Q), "v": (2, C_V)}[n]
                now(ve, u, f"tap_{n}" if j == 1 else f"cv{j - 1}_{n}")
                a = acc[:, i, :].rearrange("p (b t) -> p b t", b=NB)[:, :, j:T]
                s = bconv[i][:, :].rearrange("p (b t) -> p b t", b=NB)[:, :, 0:T - j]
                STT(a, s, sm[:, c0 + 3 - j:c0 + 4 - j], a, ALU.mult, ALU.add).then_inc(S[f"cv{j}_{n}"], 1)

            def silu(u, i):
                n = "kqv"[i]
                now(ve, u, f"tanh_{n}")
                if i == 0:
                    before(ve, u, "diag_mm", "lv1_mm", "kl2", "kl_odd", "ksq_ok", "kq1")
                elif i == 1:
                    before(ve, u, "diag_mm", "kq1", "qsq_ok")
                else:
                    before(ve, u, "vT_mm")
                dst = vv[:, :] if i == 2 else kq[:, i, :]
                STT(dst, th[:, i, :], 1.0, acc[:, i, :], ALU.add, ALU.mult).then_inc(S[f"silu_{n}"], 1)

            def first(u):
                now(ve, u, "g_ready", "silu_k", "silu_q")
                before(ve, u, "lv128_mm")
                TT2(KQ[:, :, :], kq[:, :, :], G[1][:, :].unsqueeze(1).to_broadcast([P, 2, TOK]), ALU.mult)\
                    .then_inc(S["kq1"], 1)

            def first_columns(bnk):
                return bnk[:, 0:NC * H].rearrange("p (c s) -> p c s", c=NC)[:, :, 0]

            def norms(u, p):
                now(ve, u, "ssk_mm")
                before(ve, u, "nh_ok")
                TS(ssk[:, :], first_columns(bM), QK_EPS, None, ALU.add)
                TS(ssk4[:, :], first_columns(bM), QK_EPS, 0.25, ALU.add, ALU.mult).then_inc(S["ssk_ok"], 1)
                now(ve, u, "ssk_ok")
                nc.vector.reciprocal(rec[:, :], ssk[:, :]).then_inc(S["rec_ok"], 1)
                now(ve, u, "rec_ok")
                older(ve, u, "u1_ok")
                before(ve, u, "mb2", "k64_ok")
                TT2(b2[p][:, :], beta[:, u.h, :], rec[:, :], ALU.mult)
                STT(b2n[:, :], beta[:, u.h, :], -1.0, rec[:, :], ALU.mult, ALU.mult).then_inc(S["b2_ok"], 1)

            def up(u, h):
                now(ve, u, f"lv{h}_mm", f"kq{h}")
                if h < 64:
                    o = halves(KQ[:, :, :], h)[:, :, :, 1, :]
                    g = halves(G[h][:, :], 1)[:, :, 0, :]
                    g = g.unsqueeze(1).to_broadcast([P, 2, TOK // (2 * h), h])
                else:
                    o = KQ[:, :, :].rearrange("p k (b f t) -> p k b f t", b=NB, f=4)[:, :, :, 3, :]
                    g = G[64][:, :].rearrange("p (b f) -> p b f", b=NB)[:, :, 2:3]
                    g = g.unsqueeze(1).to_broadcast([P, 2, NB, 64])
                TT2(o, o, g, ALU.mult).then_inc(S[f"kq{2 * h}"], 1)

            def masks_0(u, p):
                now(ve, u, "diag_mm")
                older(ve, u, "o_mm")
                TT2(AQ[p][:, :, :], bA[:, :].rearrange("p (c s) -> p c s", c=NC),
                    const(K_ID, P).unsqueeze(1).to_broadcast([P, NC, P]), ALU.mult).then_inc(S["ev0"], 1)

            def masks(u, p, h):
                n = LEVELS.index(h)
                now(ve, u, f"lv{h}_mm", f"mb{n // 2}", f"ev{h // 2}")
                older(ve, u, "t1_mm" if h == 1 else f"m{h}_mm")
                src = level_bank[h][:, 0:NC * H].rearrange("p (c k n h) -> p c k n h", c=NC, k=2, h=h)
                TT2(halves(L[p][:, n, :, :], h)[:, :, :, 1, :], src[:, :, 0, :, :],
                    mb[:, n, :, :].rearrange("p c (n h) -> p c n h", h=h), ALU.mult)
                for s in range(2):
                    r = slice(s * H, (s + 1) * H)
                    m = cst[r, K_SM + SB * n:K_SM + SB * (n + 1)].bitcast(U32).rearrange("p (n h) -> p n h", h=h)\
                        .unsqueeze(1).to_broadcast([H, NC, SB // h, h])
                    last = nc.vector.copy_predicated(halves(AQ[p][r, :, r], h)[:, :, :, 1, :], m, src[r, :, 1, :, :])
                last.then_inc(S[f"ev{h}"], 1)

            def masks64(u, p):
                now(ve, u, "lv64_mm", "b2_ok")
                older(ve, u, "m64_mm")
                TT2(LT64[p][0:64, :, :], bB[0:64, :].rearrange("p (c k s) -> p c k s", c=NC, k=2)[:, :, 0, :],
                    b2n[0:64, :].unsqueeze(2).to_broadcast([64, NC, 64]), ALU.mult).then_inc(S["k64_ok"], 1)

            def inv_first(u, p):
                before(ve, u, "u1_mm")
                TT2(Tt[:, :, :], L[p][:, 0, :, :], const(K_ID64, H).unsqueeze(1).to_broadcast([P, NC, H]), ALU.add)\
                    .then_inc(S["tt1"], 1)

            def inv_t1(u, c):
                now(ve, u, "t1_mm")
                if c:
                    now(ve, c, "ssk_mm")
                before(ve, u, "m64_mm")
                TT2(Tm[:, :, :], bM[:, NC * H:2 * NC * H].rearrange("p (c s) -> p c s", c=NC),
                    const(K_ID64, H).unsqueeze(1).to_broadcast([P, NC, H]), ALU.add).then_inc(S["t1_ok"], 1)

            def inv_t(u, h):
                now(ve, u, f"t{h}_mm", f"t{h // 2}_ok", f"s{h // 2}_ok" if h > 2 else "tt1")
                for t, bnk, half, name in ((Tm, bT, 0, "t"), (Tt, bS, 1, "s")):
                    cols = halves(t[:, :, :], h)[:, :, :, half, :]
                    TT2(cols, halves(bnk[:, 0:NC * H].rearrange("p (c s) -> p c s", c=NC), h)[:, :, :, half, :], cols,
                        ALU.add).then_inc(S[f"{name}{h}_ok"], 1)

            def cross(u, p):
                now(ve, u, "x_mm")
                before(ve, u, "u1_mm")
                TT2(R[:, :, :], Vn[p][:, :, :].rearrange("p (b two) v -> p b two v", two=2)[:, :, 1, :],
                    bM[:, 2 * P:4 * P].rearrange("p (b v) -> p b v", b=NB), ALU.subtract).then_inc(S["r_ok"], 1)

            def gate_out(u):
                now(ve, u, "osq_ok", "sg_ok")
                before(ve, u, "og_ok")
                STT(OGr[:, :], sg[:, :], 1.0, bS[:, :], ALU.add, ALU.mult).then_inc(S["og_raw"], 1)

            def out_norms(u):
                now(ve, u, "st_mm")
                before(ve, u, "rr_ok")
                TS(st[:, :], first_columns(bT), P * O_EPS * QK_EPS, None, ALU.add).then_inc(S["st_ok"], 1)

            def scale_out(u):
                now(ve, u, "rb_mm", "og_raw")
                TT2(OG[:, u.h, :], OGr[:, :], bT[:, :], ALU.mult).then_inc(S["og_ok"], 1)

            def step(a, b, c, d, p):
                if c:
                    gate_min(c)
                if d:
                    scale_out(d)
                masks(a, p, 1)
                fill = {2: ("", "k1"), 4: ("k2", "g"), 8: ("k3", "q1"), 16: ("q2", "q3"), 32: ("0", "1")}

                def between(what):
                    if what == "g":
                        gate_max(c)
                    elif what in ("0", "1"):
                        silu(c, int(what))
                    elif what:
                        conv(c, what[0], int(what[1]))

                for h in LEVELS[1:]:
                    up(a, h)
                    if c:
                        between(fill[h][0])
                    if b:
                        inv_t(b, h)
                    masks(a, p, h)
                    if h == 2:
                        silu(a, 2)
                    if c:
                        between(fill[h][1])
                up(a, 64)
                masks64(a, p)
                if c:
                    first(c)
                if b:
                    cross(b, 1 - p)
                if c:
                    for j in (1, 2, 3):
                        conv(c, "v", j)
                if c:
                    up(c, 1)
                if b:
                    gate_out(b)
                inv_first(a, p)
                if c:
                    norms(c, 1 - p)
                inv_t1(a, c)
                if b:
                    out_norms(b)
                if c:
                    masks_0(c, 1 - p)

            def expert(g, gu, e, b):
                ve.wait_ge(S["ffn_tanh"], g * ET + e + 1)
                STT(fu[:, :], ftan[:, :], 1.0, ffn_banks[e % 2][0][:, :], ALU.add, ALU.mult).then_inc(S["ffn_u"], 1)
                ve.wait_ge(S["ffn_u"], g * ET + e + 1)
                if e == 0:
                    before(ve, gu, "group_mm")
                    now(ve, b, "qsq_ok", "kl_odd", "diag_mm", "lv1_mm", "kl2")
                STT(hid[:, e, :], fu[:, :], hidscale[:, 0:1], ffn_banks[e % 2][1][:, :], ALU.mult, ALU.mult)\
                    .then_inc(S["ffn_hid"], 1)

            def last_head(g, gu, b, d):
                scale_out(d)
                for e, h in enumerate(LEVELS[1:]):
                    expert(g, gu, e, b)
                    inv_t(b, h)
                expert(g, gu, 5, b)
                expert(g, gu, 6, b)
                cross(b, 1)
                expert(g, gu, 7, b)
                gate_out(b)
                out_norms(b)
                scale_out(b)

            for t in (L[0], L[1], Tx):
                last = nc.vector.memset(t[:], 0.0)
            last.then_inc(S["zero_ok"], 1)
            ve.wait_ge(S["wsum_ok"], 3)
            ve.wait_ge(S["wsum_mm"], 1)
            ve.wait_ge(S["zero_ok"], 1)
            TS(wscale[:, :], bX[:, 0:3], 1.0 / (HID * EXP), 1e-8, ALU.mult, ALU.add).then_inc(S["setup_v"], 1)
            ve.wait_ge(S["setup_v"], 1)
            TS(wthr[:, 0:3], wscale[:, :], 0.5, None, ALU.mult)
            TS(wthr[:, 3:6], wscale[:, :], -0.5, None, ALU.mult).then_inc(S["setup_v"], 1)
            ve.wait_ge(S["setup_v"], 2)
            n = 2
            for i, w in enumerate((wup, wgt, wdn)):
                flat = w[:, :, :].rearrange("p a b -> p (a b)")
                TS(tern[:, :], flat, wthr[:, i:i + 1], None, ALU.is_gt)
                TS(tern2[:, :], flat, wthr[:, 3 + i:4 + i], None, ALU.is_lt).then_inc(S["setup_v"], 1)
                n += 1
                ve.wait_ge(S["setup_v"], n)
                TT2(flat, tern[:, :], tern2[:, :], ALU.subtract).then_inc(S["setup_v"], 1)
                n += 1
                ve.wait_ge(S["setup_v"], n)
            TS(upscale[:, :], wscale[:, 0:1], 0.5, None, ALU.mult)
            TT2(hidscale[:, :], wscale[:, 0:1], wscale[:, 1:2], ALU.mult).then_inc(S["setup_v"], 1)
            n += 1
            ve.wait_ge(S["setup_v"], n)
            STT(hidscale[:, :], hidscale[:, :], 0.5, wscale[:, 2:3], ALU.mult, ALU.mult)
            TS(wo[:, :, :], wo[:, :, :], nw[:, 0:1], 0.5, ALU.mult, ALU.mult)
            ve.wait_ge(S["a_exp"], 1)
            TS(smalls[:, :, C_A], smalls[:, :, C_A], -1.0, None, ALU.mult).then_inc(S["setup_ok"], 1)

            with ve.Fori(0, groups) as g:
                gu = Unit(ve, g)
                ve.wait_ge(S["x_in"], gu.dma)
                before(ve, gu, "mv_ok")
                for c in range(NC):
                    last = nc.vector.bn_stats(bst[:, c, :], xt[:, c, :])
                last.then_inc(S["bn_ok"], 1)
                constant_wait(ve)
                now(ve, gu, "bn_ok")
                before(ve, gu, "xn_ok")
                for c in range(NC):
                    last = nc.vector.bn_aggr(mv[:, c, :], bst[:, c, :])
                last.then_inc(S["mv_ok"], 1)
                now(ve, gu, "rstd_ok")
                before(ve, gu, "xT_mm")
                for c in range(NC):
                    last = TS(xn[:, c, :], xt[:, c, :], mv[:, c, 0:1], rstd[:, c:c + 1], ALU.subtract, ALU.mult)
                last.then_inc(S["xn_ok"], 1)
                now(ve, gu, "beta_exp")
                TS(beta[:, :, :], beta[:, :, :], 1.0, None, ALU.add).then_inc(S["beta_1"], 1)
                now(ve, gu, "beta_1")
                nc.vector.reciprocal(beta[:, :, :], beta[:, :, :]).then_inc(S["beta_ok"], 1)
                now(ve, gu, "beta_ok")
                first_head = Unit(ve, g * HEADS, 0)
                gate_min(first_head)
                gate_max(first_head)
                for n in "kqv":
                    for j in (1, 2, 3):
                        conv(first_head, n, j)
                for i in range(2):
                    silu(first_head, i)
                first(first_head)
                norms(first_head, 0)
                up(first_head, 1)
                masks_0(first_head, 0)
                pipeline(ve, g, step, lambda b, d: last_head(g, gu, b, d))
                now(ve, gu, "group_mm")
                ve.wait_ge(S["out_done"], gu.dma)
                for i in range(2):
                    last = TT2(ot[:, 2 * i:2 * i + 2, :], (bT, bS)[i][:, :].rearrange("p (c n) -> p c n", c=2),
                               xres[:, 2 * i:2 * i + 2, :], ALU.add)
                last.then_inc(S["out_ok"], 1)

        @block.gpsimd
        def _(gp):
            GT = nc.gpsimd.tensor_tensor
            prime(gp, "POOL")

            def small_cols(u):
                constant_wait(gp)
                before(gp, u, "cv3_k", "cv3_q", "cv3_v", "g_ready")
                nc.gpsimd.tensor_copy(sm[:, :], smalls[:, u.h, :]).then_inc(S["sm_ok"], 1)

            def up(u, h):
                if h == 1:
                    now(gp, u, "g_ready", "silu_k")
                    before(gp, u, "lv128_mm", "kq4", "kl4")
                else:
                    now(gp, u, f"lv{h}_mm", f"kl{h}")
                    if h < 64:
                        before(gp, u, f"kq{4 * h}", f"kl{4 * h}")
                if h < 64:
                    g2 = halves(G[h][:, :], 1)
                    GT(G[2 * h][:, :].unsqueeze(2), g2[:, :, 0, :], g2[:, :, 1, :], ALU.mult)
                    o = halves(KL[:, :], h)[:, :, 0, :]
                    s = halves(kq[:, 0, :], h)[:, :, 0, :] if h == 1 else o
                    g = g2[:, :, 1, :].to_broadcast([P, TOK // (2 * h), h])
                else:
                    o = KL[:, :].rearrange("p (b f t) -> p b f t", b=NB, f=4)[:, :, 0, :]
                    s = o
                    g = G[64][:, :].rearrange("p (b f) -> p b f", b=NB)[:, :, 1:2].to_broadcast([P, NB, 64])
                GT(o, s, g, ALU.mult).then_inc(S[f"kl{2 * h}"], 1)

            def norms(u):
                now(gp, u, "ssk_ok")
                before(gp, u, "v_norm")
                GT(nh[:, :], ssk4[:, :], const(K_HALF, NC), ALU.pow).then_inc(S["nh_ok"], 1)

            def scaled_masks(u, i):
                now(gp, u, "b2_ok")
                before(gp, u, f"ev{LEVELS[2 * i + 1]}")
                for n in (2 * i, 2 * i + 1):
                    last = GT(mb[:, n, :, :], const(K_SM + SB * n, SB).unsqueeze(1).to_broadcast([P, NC, SB]),
                              b2n[:, :].unsqueeze(2).to_broadcast([P, NC, SB]), ALU.mult)
                last.then_inc(S[f"mb{i}"], 1)

            def scales(u):
                now(gp, u, "st_ok")
                before(gp, u, "rb_mm")
                GT(rr[:, :], st[:, :], const(K_NHALF, NC), ALU.pow).then_inc(S["rr_ok"], 1)

            def step(a, b, c, d, p):
                if c:
                    small_cols(c)
                if a:
                    scaled_masks(a, 0)
                    up(a, 2)
                    scaled_masks(a, 1)
                    up(a, 4)
                    scaled_masks(a, 2)
                    for h in (8, 16, 32, 64):
                        up(a, h)
                if c:
                    up(c, 1)
                if b:
                    scales(b)
                if c:
                    norms(c)

            gp.wait_ge(S["setup_ok"], 1)
            with gp.Fori(0, groups) as g:
                gu = Unit(gp, g)
                constant_wait(gp)
                now(gp, gu, "mv_ok")
                before(gp, gu, "xn_ok")
                nc.gpsimd.tensor_scalar(rstd[:, :], mv[:, :, 1], LN_EPS, None, ALU.add).then_inc(S["rstd_e"], 1)
                gp.wait_ge(S["rstd_e"], g + 1)
                GT(rstd[:, :], rstd[:, :], const(K_NHALF, NC), ALU.pow).then_inc(S["rstd_ok"], 1)
                first_head = Unit(gp, g * HEADS, 0)
                small_cols(first_head)
                up(first_head, 1)
                norms(first_head)
                pipeline(gp, g, step, lambda b, d: scales(b))


def kernel(L0_attn_hidden_states, L0_attn_Wq, L0_attn_Wk, L0_attn_Wv, L0_attn_conv_q, L0_attn_conv_k,
           L0_attn_conv_v, L0_attn_A_log, L0_attn_Wfa, L0_attn_Wfb, L0_attn_dt_bias, L0_attn_Wb, L0_attn_Wga,
           L0_attn_Wgb, L0_attn_norm_w, L0_attn_Wo, L0_ffn_W_up, L0_ffn_W_gate, L0_ffn_W_down):
    import concourse.bacc as bacc
    from concourse.bass_utils import run_bass_kernel_spmd

    f = np.asarray
    x = f(L0_attn_hidden_states)
    groups = x.shape[0] // NB

    xg = x.reshape(groups, NC, P, HID).transpose(0, 2, 1, 3)

    def head_tiles(w):
        return f(w).reshape(-1, P, HEADS, P).transpose(2, 1, 0, 3)

    wh = np.concatenate([head_tiles(L0_attn_Wfb), head_tiles(L0_attn_Wk), head_tiles(L0_attn_Wq),
                         head_tiles(L0_attn_Wv)], axis=2).reshape(HEADS, P, WCOLS)
    wgb = head_tiles(L0_attn_Wgb).reshape(HEADS, P, P)
    small = np.zeros((P, HEADS, 16), np.float32)
    for c0, w in ((C_Q, L0_attn_conv_q), (C_K, L0_attn_conv_k), (C_V, L0_attn_conv_v)):
        small[:, :, c0:c0 + TAPS] = f(w).reshape(HEADS, P, TAPS).transpose(1, 0, 2)
    small[:, :, C_DT] = f(L0_attn_dt_bias).reshape(HEADS, P).T
    small[:, :, C_A] = np.broadcast_to(f(L0_attn_A_log).reshape(1, HEADS), (P, HEADS))

    def rows(w):
        return f(w).reshape(-1, P, w.shape[1]).transpose(1, 0, 2)

    arrays = {
        "x": xg, "wh": wh, "wgb": wgb, "small": small,
        "wfg": np.stack([rows(L0_attn_Wfa), rows(L0_attn_Wga)], axis=1),
        "wb": rows(L0_attn_Wb), "wo": rows(L0_attn_Wo), "nw": f(L0_attn_norm_w).reshape(P, 1),
        "wup": rows(f(L0_ffn_W_up).T), "wgt": rows(f(L0_ffn_W_gate).T), "wdn": rows(f(L0_ffn_W_down).T),
        "const": constants(),
    }
    arrays = {n: np.ascontiguousarray(a) for n, a in arrays.items()}
    nc = bacc.Bacc("TRN2", target_bir_lowering=False, num_devices=1)
    args = [nc.dram_tensor(f"{n}_dram", a.shape, F32, kind="ExternalInput").ap() for n, a in arrays.items()]
    out = nc.dram_tensor("out_dram", (groups, P, NC, HID), F32, kind="ExternalOutput").ap()
    build(nc, *args, out)
    r = run_bass_kernel_spmd(nc, [{f"{n}_dram": a for n, a in arrays.items()}], core_ids=[0])
    y = np.asarray(r.results[0]["out_dram"])
    return y.transpose(0, 2, 1, 3).reshape(x.shape)
```

```python
from contextlib import ExitStack

import numpy as np

import concourse.bass as bass
from concourse import mybir

F32 = mybir.dt.float32
F32R = mybir.dt.float32r
U32 = mybir.dt.uint32
ALU = mybir.AluOpType
ACT = mybir.ActivationFunctionType
AX = mybir.AxisListType

P = 128
NB = 2
T = 256
TOK = NB * T
NC = TOK // P
HEADS = 16
HID = 256
KT = HID // P
EXP = 1024
ET = EXP // P
SB = 32
H = P // 2
TAPS = 4
LEVELS = (1, 2, 4, 8, 16, 32)
NLEV = len(LEVELS)

W_F, W_K, W_Q, W_V = 0, 1, 3, 5
WCOLS = 7 * P
C_Q, C_K, C_V, C_DT, C_A, C_N = 0, 4, 8, 12, 13, 14

K_ID = 0
K_ID64 = K_ID + P
K_SM = K_ID64 + H
K_OSC = K_SM + NLEV * SB
K_HALF = K_OSC + H
K_NHALF = K_HALF + NC
K_ONES = K_NHALF + NC
K_COLS = K_ONES + P

LN_EPS = 1e-5
QK_EPS = 4e-6
O_EPS = 1e-6
Q_WEIGHT = P * O_EPS ** 0.5


def constants():
    c = np.zeros((P, K_COLS), np.float32)
    i = np.arange(P)
    c[i, K_ID + i] = 1
    c[i, K_ID64 + i % H] = 1
    for n, h in enumerate(LEVELS):
        for j in range(SB):
            t = (j // h) * 2 * h + h + j % h
            c[:, K_SM + SB * n + j] = (i % H // (2 * h) == t // (2 * h)) & (i % (2 * h) < h)
    c[:, K_OSC:K_OSC + H] = 1.0 / P
    c[:, K_HALF:K_HALF + NC] = 0.5
    c[:, K_NHALF:K_NHALF + NC] = -0.5
    c[:, K_ONES:K_ONES + P] = 1.0
    return c


def build(nc, x_d, wh_d, wgb_d, sm_d, wfg_d, wb_d, wo_d, nw_d, wup_d, wgt_d, wdn_d, const_d, out_d):
    groups = x_d.shape[0]
    ctx = ExitStack()
    with ctx:
        def sb(name, shape, dt=F32):
            return ctx.enter_context(nc.sbuf_tensor(name, shape, dt))

        def bank(name):
            return ctx.enter_context(nc.psum_tensor(name, [P, 512], F32))

        cst = sb("cst", [P, K_COLS])
        smalls = sb("smalls", [P, HEADS, 16])
        wfg = sb("wfg", [P, 2, KT, P])
        wb = sb("wb", [P, KT, HEADS])
        wo = sb("wo", [P, HEADS, HID])
        nw = sb("nw", [P, 1])
        wup = sb("wup", [P, KT, EXP], F32R)
        wgt = sb("wgt", [P, KT, EXP], F32R)
        wdn = sb("wdn", [P, ET, HID])
        flat_down = wdn[:, :, :].rearrange("p a b -> p (a b)")
        wsum = sb("wsum", [P, 3])
        wscale = sb("wscale", [P, 3])
        wthr = sb("wthr", [P, 6])
        upscale = sb("upscale", [P, 1])
        hidscale = sb("hidscale", [P, 1])
        xt = sb("xt", [P, NC, HID])
        xn = sb("xn", [P, NC, HID])[:, :, :]
        bst = sb("bst", [P, NC, 6])
        mv = sb("mv", [P, NC, 2])
        rstd = sb("rstd", [P, NC])
        xnT = xn.rearrange("p c n -> p (c n)").rearrange("p (t k) -> p t k", t=KT)
        xh = sb("xh", [P, KT, TOK], F32R)
        xl = sb("xl", [P, KT, TOK], F32R)
        fh = sb("fh", [P, TOK], F32R)
        fl = sb("fl", [P, TOK], F32R)
        gaT = sb("gaT", [P, TOK])
        beta = sb("beta", [P, HEADS, NC])
        OG = sb("OG", [P, HEADS, TOK])
        tern = OG[:, 0:4, :].rearrange("p a b -> p (a b)")
        tern2 = OG[:, 4:8, :].rearrange("p a b -> p (a b)")
        wup_in, wgt_in = (OG[:, i:i + 4, :].rearrange("p a b -> p (a b)") for i in (8, 12))
        work = sb("work", [P, ET, TOK])
        acc, th, kq, hid = work[:, 0:3, :], work[:, 3:6, :], work[:, 6:8, :], work
        xres = sb("xres", [P, NC, HID])
        ot = sb("ot", [P, NC, HID])
        wraw = sb("wraw", [P, WCOLS])
        whi = [sb(f"whi{p}", [P, WCOLS], F32R) for p in range(2)]
        wlo = [sb(f"wlo{p}", [P, WCOLS], F32R) for p in range(2)]
        wgb = sb("wgb", [P, P])
        sm = sb("sm", [P, 16])
        gbuf = sb("gbuf", [P, TOK])
        vv = sb("vv", [P, TOK])
        G = {1 << n: sb(f"G{1 << n}", [P, TOK >> n]) for n in range(7)}
        KQ = sb("KQ", [P, 2, TOK])
        ftan, fu = KQ[:, 0, :], KQ[:, 1, :]
        KL = sb("KL", [P, TOK])
        ksq = sb("ksq", [P, TOK])
        ssk = sb("ssk", [P, NC])
        ssk4 = sb("ssk4", [P, NC])
        rec = sb("rec", [P, NC])
        b2n = sb("b2n", [P, NC])
        nh = sb("nh", [P, NC])
        mb = sb("mb", [P, NLEV, NC, SB])
        qsq = [sb(f"qsq{p}", [P, TOK]) for p in range(2)]
        b2 = [sb(f"b2_{p}", [P, NC]) for p in range(2)]
        L = [sb(f"L{p}", [P, NLEV, NC, H]) for p in range(2)]
        LT64 = [sb(f"LT64_{p}", [P, NC, 64]) for p in range(2)]
        AQ = [sb(f"AQ{p}", [P, NC, P]) for p in range(2)]
        AXc = [sb(f"AX{p}", [P, NB, 2 * P]) for p in range(2)]
        Vn = [sb(f"Vn{p}", [P, NC, P]) for p in range(2)]
        Tm = sb("Tm", [P, NC, H])
        Tt = sb("Tt", [P, NC, H])
        M = sb("M", [P, NC, H])
        Tx = sb("Tx", [P, NC, P])
        M64 = sb("M64", [P, NC, 64])
        R = sb("R", [P, NB, P])
        U = sb("U", [P, NC, P])
        sg = sb("sg", [P, TOK])
        OGr = sb("OGr", [P, TOK])
        osq = sb("osq", [P, TOK])
        st = sb("st", [P, NC])
        rr = sb("rr", [P, NC])

        bX, bY, bG, bA, bB, bT, bS, bM = [bank(f"bank{i}") for i in range(8)]
        bconv = [bX, bY, bX]
        ffn_banks = ((bX, bY), (bG, bA))
        level_bank = {1: bB, 2: bA, 4: bB, 8: bA, 16: bB, 32: bA}

        S = {}

        PER_HEAD = {
            "PE": ["proj_g", "proj_k", "proj_q", "proj_v", "ssk_mm", "diag_mm", "vT_mm",
                   "lv1_mm", "lv2_mm", "lv4_mm", "lv8_mm", "lv16_mm", "lv32_mm", "lv64_mm", "lv128_mm",
                   "t1_mm", "m2_mm", "m4_mm", "m8_mm", "m16_mm", "t2_mm", "t4_mm", "t8_mm", "t16_mm",
                   "m32_mm", "t32_mm", "m64_mm", "t64_mm", "u0_mm", "x_mm", "u1_mm", "o_mm", "st_mm",
                   "rb_mm", "gg_mm"],
            "ACT": ["tap_k", "tap_q", "tap_v", "g_exp", "g_ln", "g_ready", "tanh_k", "tanh_q", "tanh_v",
                    "ksq_ok", "v_norm", "q64_ok", "ax_ok",
                    "m2_ok", "m4_ok", "m8_ok", "m16_ok", "m32_ok", "m64_ok", "t64_ok", "u0_ok", "u1_ok", "osq_ok", "sg_ok",
                    "wh_hi"],
            "DVE": ["g_min", "g_max"] + [f"cv{j}_{n}" for j in (1, 2, 3) for n in "kqv"]
                   + ["silu_k", "silu_q", "silu_v", "ssk_ok", "rec_ok", "b2_ok", "kq1", "kq2", "kq4", "kq8",
                      "kq16", "kq32", "kq64", "kq128", "ev0", "ev1", "ev2", "ev4", "ev8", "ev16", "ev32",
                      "k64_ok", "t1_ok", "t2_ok", "t4_ok", "t8_ok", "t16_ok", "s2_ok", "s4_ok", "s8_ok", "s16_ok", "s32_ok", "r_ok", "og_raw", "os_ok", "st_ok",
                      "og_ok"],
            "POOL": ["wh_lo", "sm_ok", "kl2", "kl4", "kl8", "kl16", "kl32", "kl64", "kl128", "nh_ok",
                     "mb0", "mb1", "mb2", "rr_ok"],
        }
        PER_GROUP = {
            "PE": ["xT_mm", "fg_mm", "beta_mm", "down_mm", "group_mm"],
            "ACT": ["xT_ok", "xh_ok", "ga_ok", "beta_exp", "res_ok"],
            "DVE": ["bn_ok", "mv_ok", "xn_ok", "beta_1", "beta_ok", "xl_ok", "fl_ok", "out_ok"],
            "POOL": ["rstd_ok"],
        }

        ONCE = ["const_in", "x_in", "w_in", "wgb_in", "out_done", "wsum_ok", "wsum_mm", "setup_v",
                "setup_ok", "rstd_e", "ffn_mm", "ffn_tanh", "ffn_u", "ffn_hid"]
        for names in (*PER_HEAD.values(), *PER_GROUP.values(), ONCE):
            for name in names:
                S[name] = ctx.enter_context(nc.semaphore(name))

        def prime(eng, who):
            for name in PER_HEAD[who] + PER_GROUP[who]:
                eng.sem_inc(S[name], 2)

        class Unit:
            def __init__(self, eng, n, h=None):
                self.n, self.h = n, h
                self.now, self.before, self.older, self.dma = n + 3, n + 2, n + 1, n * 16 + 16
                if not isinstance(n, int):
                    self.now, self.before, self.older = (eng.snap(v) for v in (self.now, self.before, self.older))
                    for v in (self.now, self.before, self.older):
                        eng.compute_val(v)
                    if eng in (nc.sync, nc.tensor, nc.scalar):
                        self.dma = eng.snap(self.dma)
                        eng.compute_val(self.dma)

        def now(eng, u, *names):
            for n in names:
                eng.wait_ge(S[n], u.now)

        def before(eng, u, *names):
            for n in names:
                eng.wait_ge(S[n], u.before)

        def older(eng, u, *names):
            for n in names:
                eng.wait_ge(S[n], u.older)

        def pipeline(eng, g, step, more):
            def units(h0, n):
                return [Unit(eng, g * HEADS + h0 + i, h0 + i) for i in range(n)]

            u = units(0, 4)
            step(u[0], None, u[1], None, u[2], 0)
            step(u[1], u[0], u[2], None, u[3], 1)
            with eng.Fori(0, HEADS // 2 - 2) as i:
                v = units(2 * i, 6)
                step(v[2], v[1], v[3], v[0], v[4], 0)
                step(v[3], v[2], v[4], v[1], v[5], 1)
            u = units(HEADS - 4, 6 if more else 4) + [None, None]
            step(u[2], u[1], u[3], u[0], u[4], 0)
            step(u[3], u[2], None, u[1], u[5], 1)
            return u[3], u[2]

        def all_groups(eng, group):
            if groups > 1:
                with eng.Fori(0, groups - 1) as g:
                    group(g, True)
            group(groups - 1, False)

        def constant_wait(eng):
            eng.wait_ge(S["setup_ok"], 1)

        def halves(ap, h):
            d = " ".join(f"a{i}" for i in range(len(ap.shape) - 1))
            return ap.rearrange(f"{d} (n two h) -> {d} n two h", two=2, h=h)

        def chunk_halves():
            return [(c, c * P + s * H, slice(s * H, (s + 1) * H)) for c in range(NC) for s in range(2)]

        def const(c0, n):
            return cst[:, c0:c0 + n]

        block = ctx.enter_context(nc.Block())

        @block.sync
        def _(sp):
            sp.sem_inc(S["out_done"], 16)
            for dst, src in ((cst[:, :], const_d), (wup_in, wup_d), (wgt_in, wgt_d),
                             (wdn[:, :, :], wdn_d), (smalls[:, :, :], sm_d), (wfg[:, :, :, :], wfg_d),
                             (wb[:, :, :], wb_d), (wo[:, :, :], wo_d), (nw[:, :], nw_d)):
                sp.dma_start(dst, src).then_inc(S["const_in"], 16)

            def load_x(g, gu):
                before(sp, gu, "xn_ok", "res_ok")
                sp.dma_start(xt[:, :, :], x_d[g]).then_inc(S["x_in"], 16)

            def load_w(u, h):
                before(sp, u, "wh_lo")
                sp.dma_start(wraw[:, :], wh_d[h]).then_inc(S["w_in"], 16)

            def load_wgb(u, h):
                before(sp, u, "gg_mm")
                sp.dma_start(wgb[:, :], wgb_d[h]).then_inc(S["wgb_in"], 16)

            def group(g, more):
                gu = Unit(sp, g)
                if more:
                    load_x(g + 1, Unit(sp, g + 1))
                with sp.Fori(0, HEADS - 2) as j:
                    load_w(Unit(sp, g * HEADS + j + 2), j + 2)
                    load_wgb(Unit(sp, g * HEADS + j), j)
                for i in range(2):
                    if more:
                        load_w(Unit(sp, g * HEADS + HEADS + i), i)
                    load_wgb(Unit(sp, g * HEADS + HEADS - 2 + i), HEADS - 2 + i)
                now(sp, gu, "out_ok")
                sp.dma_start(out_d[g], ot[:, :, :]).then_inc(S["out_done"], 16)

            load_x(0, Unit(sp, 0))
            for i in range(2):
                load_w(Unit(sp, i), i)
            all_groups(sp, group)
            sp.wait_ge(S["out_done"], 16 * groups + 16)

        @block.tensor
        def _(pe):
            mm = nc.tensor.matmul
            prime(pe, "PE")

            def three(bnk, w, hi, lo, p, first, last):
                cols = slice(w * P, (w + 1) * P)
                mm(bnk[:, :], whi[p][:, cols], hi, start=first, stop=False)
                mm(bnk[:, :], whi[p][:, cols], lo, start=False, stop=False)
                return mm(bnk[:, :], wlo[p][:, cols], hi, start=False, stop=last)

            def proj_g(u, b, p):
                now(pe, u, "wh_lo")
                before(pe, u, "g_max")
                if b:
                    now(pe, b, "v_norm")
                three(bG, W_F, fh[:, :], fl[:, :], p, True, True).then_inc(S["proj_g"], 1)

            def proj(u, n, t, p):
                bnk, w0 = {"k": (bX, W_K), "q": (bY, W_Q), "v": (bX, W_V)}[n]
                if t == 0:
                    if n == "v":
                        now(pe, u, "cv3_k")
                    else:
                        before(pe, u, {"k": "cv3_v", "q": "cv3_q"}[n])
                last = three(bnk, w0 + t, xh[:, t, :], xl[:, t, :], p, t == 0, t == KT - 1)
                if t == KT - 1:
                    last.then_inc(S[f"proj_{n}"], 1)

            def key_norms(u):
                now(pe, u, "ksq_ok")
                for c in range(NC):
                    last = mm(bM[:, c * H:(c + 1) * H], ksq[:, c * P:(c + 1) * P], const(K_ONES, H), start=True, stop=True)
                last.then_inc(S["ssk_mm"], 1)

            def diagonal(u):
                now(pe, u, "silu_k", "silu_q")
                before(pe, u, "ax_ok")
                for c in range(NC):
                    last = mm(bA[:, c * P:(c + 1) * P], kq[:, 0, c * P:(c + 1) * P], kq[:, 1, c * P:(c + 1) * P],
                              start=True, stop=True)
                last.then_inc(S["diag_mm"], 1)

            def v_turn(u, b, c):
                now(pe, u, "silu_v")
                if b:
                    now(pe, b, "sg_ok")
                else:
                    now(pe, c, "g_max")
                for k in range(NC):
                    last = nc.tensor.transpose(bG[:, k * P:(k + 1) * P], vv[:, k * P:(k + 1) * P], const(K_ID, P))
                last.then_inc(S["vT_mm"], 1)

            def level(u, h):
                bnk = level_bank[h]
                left = kq[:, 0, :] if h == 1 else KL[:, :]
                constant_wait(pe)
                now(pe, u, f"kq{h}")
                if h > 1:
                    now(pe, u, f"kl{h}", f"ev{h // 4}")
                else:
                    before(pe, u, "q64_ok", "k64_ok")
                if h == 2:
                    now(pe, u, "ksq_ok")
                for c, t0, rows in chunk_halves():
                    right = halves(KQ[:, :, t0:t0 + H], h)[:, :, :, 1, :]
                    last = mm(bnk[rows, c * H:(c + 1) * H].rearrange("p (k n h) -> p k n h", k=2, h=h),
                              left[:, t0:t0 + H], right, start=True, stop=True)
                last.then_inc(S[f"lv{h}_mm"], 1)

            def level64(u):
                now(pe, u, "kq64", "kl64", "ev16")
                for c in range(NC):
                    last = mm(bB[0:64, c * P:(c + 1) * P].rearrange("p (k h) -> p k h", k=2),
                              KL[:, c * P:c * P + 64], KQ[:, :, c * P + 64:(c + 1) * P], start=True, stop=True)
                last.then_inc(S["lv64_mm"], 1)

            def level128(u):
                now(pe, u, "kq128", "kl128", "ev32")
                for b in range(NB):
                    last = mm(bA[:, b * T:(b + 1) * T].rearrange("p (k h) -> p k h", k=2),
                              KL[:, b * T:b * T + P], KQ[:, :, b * T + P:(b + 1) * T], start=True, stop=True)
                last.then_inc(S["lv128_mm"], 1)

            def inv_first(u, p):
                constant_wait(pe)
                now(pe, u, "ev1")
                for c, _, rows in chunk_halves():
                    last = mm(bM[rows, NC * H + c * H:NC * H + (c + 1) * H], L[p][rows, 0, c, :], cst[rows, K_ID64:K_ID64 + H],
                              start=True, stop=True)
                last.then_inc(S["t1_mm"], 1)

            def inv_m(u, p, h, a=None):
                constant_wait(pe)
                now(pe, u, f"ev{h}", f"t{h // 2}_ok")
                if h == 2 and a:
                    now(pe, a, "ssk_ok")
                for c, _, rows in chunk_halves():
                    last = mm(bM[rows, c * H:(c + 1) * H], L[p][rows, LEVELS.index(h), c, :], Tm[rows, c, :],
                              start=True, stop=True)
                last.then_inc(S[f"m{h}_mm"], 1)

            def inv_t(u, h):
                constant_wait(pe)
                now(pe, u, f"m{h}_ok", f"s{h // 2}_ok" if h > 2 else "t1_ok")
                if h == 2:
                    before(pe, u, "og_ok")
                for c, _, rows in chunk_halves():
                    mm(bT[rows, c * H:(c + 1) * H], Tt[rows, c, :], M[rows, c, :], start=True, stop=True)
                    last = mm(bS[rows, c * H:(c + 1) * H], M[rows, c, :], Tt[rows, c, :], start=True, stop=True)
                last.then_inc(S[f"t{h}_mm"], 1)

            def inv_m64(u, p):
                constant_wait(pe)
                now(pe, u, "k64_ok", "s32_ok")
                for c in range(NC):
                    last = mm(bM[64:128, c * 64:(c + 1) * 64], LT64[p][0:64, c, :], Tm[0:64, c, :],
                              start=True, stop=True)
                last.then_inc(S["m64_mm"], 1)

            def inv_t64(u):
                constant_wait(pe)
                now(pe, u, "m64_ok", "s32_ok")
                for c in range(NC):
                    last = mm(bM[0:64, 256 + c * 64:256 + (c + 1) * 64], M64[64:128, c, :], Tt[64:128, c, :],
                              start=True, stop=True)
                last.then_inc(S["t64_mm"], 1)

            def solve_0(u, p):
                now(pe, u, "t64_ok", "v_norm")
                for b in range(NB):
                    last = mm(bM[:, b * P:(b + 1) * P], Tx[:, 2 * b, :], Vn[p][:, 2 * b, :], start=True, stop=True)
                last.then_inc(S["u0_mm"], 1)

            def solve_x(u, p):
                now(pe, u, "u0_ok", "ax_ok")
                for b in range(NB):
                    last = mm(bM[:, (2 + b) * P:(3 + b) * P], AXc[p][:, b, 0:P], U[:, 2 * b, :],
                              start=True, stop=True)
                last.then_inc(S["x_mm"], 1)

            def solve_1(u):
                now(pe, u, "r_ok")
                for b in range(NB):
                    last = mm(bM[:, b * P:(b + 1) * P], Tx[:, 2 * b + 1, :], R[:, b, :], start=True, stop=True)
                last.then_inc(S["u1_mm"], 1)

            def output(u, p):
                now(pe, u, "u1_ok", "q64_ok", "ev32")
                for b in range(NB):
                    c0, c1 = 2 * b, 2 * b + 1
                    mm(bS[:, c0 * P:(c0 + 1) * P], U[:, c0, :], AQ[p][:, c0, :], start=True, stop=True)
                    mm(bS[:, c1 * P:(c1 + 1) * P], U[:, c0, :], AXc[p][:, b, P:2 * P], start=True, stop=False)
                    last = mm(bS[:, c1 * P:(c1 + 1) * P], U[:, c1, :], AQ[p][:, c1, :], start=False, stop=True)
                last.then_inc(S["o_mm"], 1)

            def gate2(u, c):
                pe.wait_ge(S["wgb_in"], u.dma)
                if c:
                    now(pe, c, "g_max")
                else:
                    now(pe, u, "v_norm")
                mm(bG[:, :], wgb[:, :], gaT[:, :], start=True, stop=True).then_inc(S["gg_mm"], 1)

            def out_norms(u):
                now(pe, u, "os_ok")
                for c in range(NC):
                    last = mm(bT[:, c * H:(c + 1) * H], osq[:, c * P:(c + 1) * P], const(K_OSC, H),
                              start=True, stop=True)
                last.then_inc(S["st_mm"], 1)

            def spread(u):
                now(pe, u, "rr_ok")
                for c in range(NC):
                    last = mm(bT[:, c * P:(c + 1) * P], rr[:, c:c + 1].to_broadcast([P, P]), const(K_ID, P),
                              start=True, stop=True)
                last.then_inc(S["rb_mm"], 1)

            def step(a, b, c, d, e, p):
                if c:
                    proj_g(c, b, 1 - p)
                fill = {2: ("k0", "k1"), 4: ("q0", "q1"), 8: ("", "v0"), 16: ("", "g"), 32: ("", "v1")}

                def dense(what):
                    if what == "g":
                        if b:
                            gate2(b, c)
                    elif what and c:
                        proj(c, what[0], int(what[1]), 1 - p)

                for h in LEVELS[1:]:
                    if b:
                        inv_m(b, 1 - p, h, a)
                    if d and h == 2:
                        spread(d)
                    if a:
                        level(a, h)
                    dense(fill[h][0])
                    if b:
                        inv_t(b, h)
                    dense(fill[h][1])
                if b:
                    inv_m64(b, 1 - p)
                if a:
                    level64(a)
                if b:
                    inv_t64(b)
                if a:
                    level128(a)
                if b:
                    solve_0(b, 1 - p)
                if a:
                    v_turn(a, b, c)
                if b:
                    solve_x(b, 1 - p)
                if c:
                    diagonal(c)
                if b:
                    solve_1(b)
                if c:
                    level(c, 1)
                if b:
                    output(b, 1 - p)
                if a:
                    inv_first(a, p)
                if c:
                    key_norms(c)
                if b:
                    out_norms(b)

            def group_turn(gu):
                now(pe, gu, "xn_ok")
                for c in range(NC):
                    for t in range(KT):
                        last = nc.tensor.transpose((bX, bY)[t][:, c * P:(c + 1) * P], xn[:, c, t * P:(t + 1) * P],
                                                   const(K_ID, P))
                last.then_inc(S["xT_mm"], 1)

            def group_gates(gu):
                now(pe, gu, "xT_ok")
                for i, bnk in enumerate((bG, bA)):
                    for t in range(KT):
                        last = mm(bnk[:, :], wfg[:, i, t, :], xnT[:, t, :], start=(t == 0), stop=(t == KT - 1))
                last.then_inc(S["fg_mm"], 1)
                for c in range(NC):
                    for t in range(KT):
                        last = mm(bB[:, c * HEADS:(c + 1) * HEADS], xnT[:, t, c * P:(c + 1) * P], wb[:, t, :],
                                  start=(t == 0), stop=(t == KT - 1))
                last.then_inc(S["beta_mm"], 1)

            def first_gate(gu, first):
                now(pe, gu, "fl_ok")
                proj_g(first, None, 0)

            def first_proj(gu, first, n):
                now(pe, gu, "xl_ok")
                for t in range(KT):
                    proj(first, n, t, 0)

            def first_products(gu, first):
                now(pe, gu, "ga_ok", "beta_exp")
                diagonal(first)
                key_norms(first)

            def expert(g, e, b):
                if e == 0:
                    now(pe, b, "cv3_k", "cv3_q", "cv3_v")
                if e == 1:
                    now(pe, b, "sg_ok", "ax_ok")
                if e >= 2:
                    pe.wait_ge(S["ffn_hid"], g * ET + e - 1)
                for bnk, w in zip(ffn_banks[e % 2], (wup, wgt)):
                    for t in range(KT):
                        for i, x in enumerate((xh, xl)):
                            last = mm(bnk[:, :], w[:, t, e * P:(e + 1) * P], x[:, t, :],
                                      start=(t == 0 and i == 0), stop=(t == KT - 1 and i == 1))
                last.then_inc(S["ffn_mm"], 1)

            def down(c):
                o = (bT, bS)[c // 2][:, (c % 2) * HID:(c % 2 + 1) * HID]
                for e in range(ET):
                    last = mm(o, hid[:, e, c * P:(c + 1) * P], wdn[:, e, :], start=(c % 2 == 0 and e == 0), stop=False)
                if c == NC - 1:
                    last.then_inc(S["down_mm"], 1)

            def heads_out(c):
                o = (bT, bS)[c // 2][:, (c % 2) * HID:(c % 2 + 1) * HID]
                for h in range(HEADS):
                    last = mm(o, OG[:, h, c * P:(c + 1) * P], wo[:, h, :], start=False,
                              stop=(c % 2 == 1 and h == HEADS - 1))
                if c == NC - 1:
                    last.then_inc(S["group_mm"], 1)

            def group(g, more):
                gu, nu = Unit(pe, g), Unit(pe, g + 1)
                before(pe, gu, "out_ok")
                b, d = pipeline(pe, g, step, more)
                gate2(b, None)
                spread(d)
                expert(g, 0, b)
                for e, h in enumerate(LEVELS[1:]):
                    inv_m(b, 1, h)
                    expert(g, e + 1, b)
                    inv_t(b, h)
                inv_m64(b, 1)
                expert(g, 6, b)
                inv_t64(b)
                solve_0(b, 1)
                expert(g, 7, b)
                solve_x(b, 1)
                if more:
                    pe.wait_ge(S["ffn_hid"], g * ET + ET - 1)
                    group_turn(nu)
                solve_1(b)
                output(b, 1)
                out_norms(b)
                pe.wait_ge(S["ffn_hid"], g * ET + ET)
                if more:
                    group_gates(nu)
                spread(b)
                now(pe, b, "og_ok")
                down(0)
                down(1)
                if more:
                    first = Unit(pe, g * HEADS + HEADS)
                    first_gate(nu, first)
                down(2)
                down(3)
                if more:
                    first_proj(nu, first, "k")
                    first_proj(nu, first, "q")
                heads_out(0)
                if more:
                    first_proj(nu, first, "v")
                heads_out(1)
                if more:
                    first_products(nu, first)
                heads_out(2)
                if more:
                    level(first, 1)
                heads_out(3)

            pe.wait_ge(S["const_in"], 16 * 9)
            pe.wait_ge(S["wsum_ok"], 3)
            mm(bX[:, 0:3], const(K_ONES, P), wsum[:, :], start=True, stop=True).then_inc(S["wsum_mm"], 1)
            pe.wait_ge(S["setup_ok"], 1)
            gu, first = Unit(pe, 0), Unit(pe, 0)
            group_turn(gu)
            group_gates(gu)
            first_gate(gu, first)
            for n in "kqv":
                first_proj(gu, first, n)
            first_products(gu, first)
            level(first, 1)
            all_groups(pe, group)

        @block.scalar
        def _(act):
            A = nc.scalar.activation
            prime(act, "ACT")

            def tap(u, n):
                i, c0 = {"k": (0, C_K), "q": (1, C_Q), "v": (2, C_V)}[n]
                now(act, u, "sm_ok", f"proj_{n}")
                before(act, u, f"silu_{n}")
                A(acc[:, i, :], bconv[i][:, :], ACT.Copy, scale=sm[:, c0 + 3:c0 + 4]).then_inc(S[f"tap_{n}"], 1)

            def gate_exp(u):
                now(act, u, "g_min")
                A(gbuf[:, :], gbuf[:, :], ACT.Exp).then_inc(S["g_exp"], 1)

            def gate_ln(u):
                now(act, u, "g_exp")
                A(gbuf[:, :], gbuf[:, :], ACT.Ln, bias=1.0).then_inc(S["g_ln"], 1)

            def gate_out(u):
                now(act, u, "g_max")
                before(act, u, "kq1", "kq2", "kl2")
                A(G[1][:, :], gbuf[:, :], ACT.Exp, scale=sm[:, C_A:C_A + 1]).then_inc(S["g_ready"], 1)

            def tanh(u, n):
                i = "kqv".index(n)
                now(act, u, f"cv3_{n}")
                before(act, u, f"silu_{n}")
                A(th[:, i, :], acc[:, i, :], ACT.Tanh, scale=0.5).then_inc(S[f"tanh_{n}"], 1)

            def key_copies(u):
                now(act, u, "silu_k")
                before(act, u, "lv128_mm")
                A(halves(KL[:, :], 1)[:, :, 1, :], halves(kq[:, 0, :], 1)[:, :, 1, :], ACT.Copy)
                before(act, u, "ssk_mm")
                A(ksq[:, :], kq[:, 0, :], ACT.Square).then_inc(S["ksq_ok"], 1)

            def query_squares(u, p):
                now(act, u, "silu_q")
                older(act, u, "st_mm")
                A(qsq[p][:, :], kq[:, 1, :], ACT.Square, scale=Q_WEIGHT)

            def v_norm(u, p):
                now(act, u, "nh_ok", "vT_mm")
                older(act, u, "u0_mm", "r_ok")
                for c in range(NC):
                    last = A(Vn[p][:, c, :], bG[:, c * P:(c + 1) * P], ACT.Copy, scale=nh[:, c:c + 1])
                last.then_inc(S["v_norm"], 1)

            def inv_m(u, h):
                now(act, u, f"m{h}_mm")
                A(M[:, :, :], bM[:, 0:NC * H].rearrange("p (c s) -> p c s", c=NC), ACT.Copy).then_inc(S[f"m{h}_ok"], 1)

            def whole_chunks(u):
                now(act, u, "s32_ok")
                before(act, u, "u1_mm")
                for r in (slice(0, H), slice(H, P)):
                    A(Tx[r, :, r], Tt[r, :, :], ACT.Copy)

            def inv_m64(u):
                now(act, u, "m64_mm")
                A(M64[64:128, :, :], bM[64:128, 0:256].rearrange("p (c s) -> p c s", c=NC), ACT.Copy)\
                    .then_inc(S["m64_ok"], 1)

            def inv_t64(u):
                now(act, u, "t64_mm")
                A(Tx[0:64, :, 64:128], bM[0:64, 256:512].rearrange("p (c s) -> p c s", c=NC), ACT.Copy)\
                    .then_inc(S["t64_ok"], 1)

            def level64(u, p):
                now(act, u, "k64_ok")
                older(act, u, "o_mm")
                A(AQ[p][0:64, :, 64:128],
                  bB[0:64, :].rearrange("p (c k s) -> p c k s", c=NC, k=2)[:, :, 1, :], ACT.Copy)\
                    .then_inc(S["q64_ok"], 1)

            def level128(u, p):
                now(act, u, "lv128_mm")
                older(act, u, "o_mm")
                A(AXc[p][:, :, :], bA[:, :].rearrange("p (b s) -> p b s", b=NB), ACT.Copy).then_inc(S["ax_ok"], 1)

            def solve(u, p, part):
                now(act, u, f"u{part}_mm")
                if part == 0:
                    before(act, u, "o_mm")
                for b in range(NB):
                    c = 2 * b + part
                    last = A(U[:, c, :], bM[:, b * P:(b + 1) * P], ACT.Copy, scale=b2[p][:, c:c + 1])
                last.then_inc(S[f"u{part}_ok"], 1)

            def gate2(u):
                now(act, u, "gg_mm")
                before(act, u, "og_raw")
                A(sg[:, :], bG[:, :], ACT.Tanh, scale=0.5).then_inc(S["sg_ok"], 1)

            def out_sq(u):
                now(act, u, "o_mm")
                before(act, u, "st_mm")
                A(osq[:, :], bS[:, :], ACT.Square).then_inc(S["osq_ok"], 1)

            def split(u, p):
                act.wait_ge(S["w_in"], u.dma)
                older(act, u, "proj_v", "wh_lo")
                A(whi[p][:, :], wraw[:, :], ACT.Copy).then_inc(S["wh_hi"], 1)

            def step(a, b, c, d, e, p):
                if a:
                    query_squares(a, p)
                if b:
                    inv_m(b, 2)
                if c:
                    gate_exp(c)
                if a:
                    tanh(a, "v")
                if c:
                    tap(c, "k")
                if b:
                    inv_m(b, 4)
                if c:
                    gate_ln(c)
                    tap(c, "q")
                if b:
                    inv_m(b, 8)
                if c:
                    gate_out(c)
                if b:
                    inv_m(b, 16)
                if c:
                    tanh(c, "k")
                if e:
                    split(e, p)
                if b:
                    gate2(b)
                    inv_m(b, 32)
                if c:
                    tanh(c, "q")
                    tap(c, "v")
                if b:
                    inv_m64(b)
                    whole_chunks(b)
                if b:
                    inv_t64(b)
                if a:
                    level64(a, p)
                if b:
                    solve(b, 1 - p, 0)
                if a:
                    level128(a, p)
                if c:
                    key_copies(c)
                if b:
                    solve(b, 1 - p, 1)
                    out_sq(b)
                if a:
                    v_norm(a, p)

            def expert(g, e):
                act.wait_ge(S["ffn_mm"], g * ET + e + 1)
                if e:
                    act.wait_ge(S["ffn_hid"], g * ET + e)
                A(ftan, ffn_banks[e % 2][0][:, :], ACT.Tanh, scale=upscale[:, 0:1]).then_inc(S["ffn_tanh"], 1)

            def turned(gu):
                now(act, gu, "xT_mm")
                for t in range(KT):
                    last = A(xnT[:, t, :], (bX, bY)[t][:, :], ACT.Copy)
                last.then_inc(S["xT_ok"], 1)

            def group_gates(gu, first):
                now(act, gu, "xT_ok")
                A(xh[:, :, :], xnT[:, :, :], ACT.Copy).then_inc(S["xh_ok"], 1)
                now(act, gu, "fg_mm")
                A(fh[:, :], bG[:, :], ACT.Copy)
                A(gaT[:, :], bA[:, :], ACT.Copy).then_inc(S["ga_ok"], 1)
                now(act, gu, "beta_mm")
                before(act, first, "b2_ok")
                A(beta[:, :, :].rearrange("p h c -> p c h"), bB[:, 0:HEADS * NC].rearrange("p (c h) -> p c h", c=NC),
                  ACT.Exp, scale=-1.0).then_inc(S["beta_exp"], 1)

            def first_head(first):
                gate_exp(first)
                gate_ln(first)
                gate_out(first)
                for n in "kqv":
                    tap(first, n)
                for n in "kq":
                    tanh(first, n)
                key_copies(first)

            def residual(gu):
                before(act, gu, "out_ok")
                A(xres[:, :, :], xt[:, :, :], ACT.Copy).then_inc(S["res_ok"], 1)

            def group(g, more):
                gu, nu = Unit(act, g), Unit(act, g + 1)
                b, d = pipeline(act, g, step, more)
                gate2(b)
                expert(g, 0)
                for e, h in enumerate(LEVELS[1:]):
                    inv_m(b, h)
                    expert(g, e + 1)
                inv_m64(b)
                whole_chunks(b)
                expert(g, 6)
                inv_t64(b)
                solve(b, 1, 0)
                expert(g, 7)
                if more:
                    turned(nu)
                solve(b, 1, 1)
                out_sq(b)
                if more:
                    first = Unit(act, g * HEADS + HEADS)
                    group_gates(nu, first)
                    now(act, gu, "down_mm")
                    first_head(first)
                    residual(nu)

            act.wait_ge(S["const_in"], 16 * 9)
            for i, w in enumerate((wup_in, wgt_in, flat_down)):
                if i:
                    act.wait_ge(S["wsum_ok"], i)
                A(tern[:, :], w, ACT.Abs,
                  accum_out=wsum[:, i:i + 1]).then_inc(S["wsum_ok"], 1)
            A(smalls[:, :, C_A], smalls[:, :, C_A], ACT.Exp).then_inc(S["wsum_ok"], 1)

            act.wait_ge(S["setup_ok"], 1)
            gu, first = Unit(act, 0), Unit(act, 0)
            turned(gu)
            for p in range(2):
                split(Unit(act, p), p)
            group_gates(gu, first)
            first_head(first)
            act.wait_ge(S["x_in"], gu.dma)
            residual(gu)
            all_groups(act, group)

        @block.vector
        def _(ve):
            TT2 = nc.vector.tensor_tensor
            TS = nc.vector.tensor_scalar
            STT = nc.vector.scalar_tensor_tensor
            prime(ve, "DVE")

            def gate_min(u):
                now(ve, u, "sm_ok", "proj_g")
                before(ve, u, "g_ready")
                TS(gbuf[:, :], bG[:, :], sm[:, C_DT:C_DT + 1], 40.0, ALU.add, ALU.min).then_inc(S["g_min"], 1)

            def gate_max(u):
                now(ve, u, "g_ln")
                STT(gbuf[:, :], bG[:, :], sm[:, C_DT:C_DT + 1], gbuf[:, :], ALU.add, ALU.max).then_inc(S["g_max"], 1)

            def conv(u, n, j):
                i, c0 = {"k": (0, C_K), "q": (1, C_Q), "v": (2, C_V)}[n]
                now(ve, u, f"tap_{n}" if j == 1 else f"cv{j - 1}_{n}")
                a = acc[:, i, :].rearrange("p (b t) -> p b t", b=NB)[:, :, j:T]
                s = bconv[i][:, :].rearrange("p (b t) -> p b t", b=NB)[:, :, 0:T - j]
                STT(a, s, sm[:, c0 + 3 - j:c0 + 4 - j], a, ALU.mult, ALU.add).then_inc(S[f"cv{j}_{n}"], 1)

            def silu(u, i):
                n = "kqv"[i]
                now(ve, u, f"tanh_{n}")
                if i == 0:
                    before(ve, u, "diag_mm", "lv1_mm", "kl2", "ksq_ok", "kq1")
                elif i == 1:
                    before(ve, u, "diag_mm", "kq1")
                else:
                    before(ve, u, "vT_mm")
                dst = vv[:, :] if i == 2 else kq[:, i, :]
                STT(dst, th[:, i, :], 1.0, acc[:, i, :], ALU.add, ALU.mult).then_inc(S[f"silu_{n}"], 1)

            def first(u):
                now(ve, u, "g_ready", "silu_k", "silu_q")
                before(ve, u, "lv128_mm")
                TT2(KQ[:, :, :], kq[:, :, :], G[1][:, :].unsqueeze(1).to_broadcast([P, 2, TOK]), ALU.mult)\
                    .then_inc(S["kq1"], 1)

            def first_columns(bnk):
                return bnk[:, 0:NC * H].rearrange("p (c s) -> p c s", c=NC)[:, :, 0]

            def norms(u, p):
                now(ve, u, "ssk_mm")
                before(ve, u, "nh_ok")
                TS(ssk[:, :], first_columns(bM), QK_EPS, None, ALU.add)
                TS(ssk4[:, :], first_columns(bM), QK_EPS, 0.25, ALU.add, ALU.mult).then_inc(S["ssk_ok"], 1)
                now(ve, u, "ssk_ok")
                nc.vector.reciprocal(rec[:, :], ssk[:, :]).then_inc(S["rec_ok"], 1)
                now(ve, u, "rec_ok")
                older(ve, u, "u1_ok")
                before(ve, u, "mb2", "k64_ok")
                TT2(b2[p][:, :], beta[:, u.h, :], rec[:, :], ALU.mult)
                STT(b2n[:, :], beta[:, u.h, :], -1.0, rec[:, :], ALU.mult, ALU.mult).then_inc(S["b2_ok"], 1)

            def up(u, h):
                now(ve, u, f"lv{h}_mm", f"kq{h}")
                if h < 64:
                    o = halves(KQ[:, :, :], h)[:, :, :, 1, :]
                    g = halves(G[h][:, :], 1)[:, :, 0, :]
                    g = g.unsqueeze(1).to_broadcast([P, 2, TOK // (2 * h), h])
                else:
                    o = KQ[:, :, :].rearrange("p k (b f t) -> p k b f t", b=NB, f=4)[:, :, :, 3, :]
                    g = G[64][:, :].rearrange("p (b f) -> p b f", b=NB)[:, :, 2:3]
                    g = g.unsqueeze(1).to_broadcast([P, 2, NB, 64])
                TT2(o, o, g, ALU.mult).then_inc(S[f"kq{2 * h}"], 1)

            def masks_0(u, p):
                now(ve, u, "diag_mm")
                older(ve, u, "o_mm")
                TT2(AQ[p][:, :, :], bA[:, :].rearrange("p (c s) -> p c s", c=NC),
                    const(K_ID, P).unsqueeze(1).to_broadcast([P, NC, P]), ALU.mult).then_inc(S["ev0"], 1)

            def masks(u, p, h):
                n = LEVELS.index(h)
                now(ve, u, f"lv{h}_mm", f"mb{n // 2}", f"ev{h // 2}")
                older(ve, u, "t1_mm" if h == 1 else f"m{h}_mm")
                src = level_bank[h][:, 0:NC * H].rearrange("p (c k n h) -> p c k n h", c=NC, k=2, h=h)
                TT2(halves(L[p][:, n, :, :], h)[:, :, :, 1, :], src[:, :, 0, :, :],
                    mb[:, n, :, :].rearrange("p c (n h) -> p c n h", h=h), ALU.mult)
                for s in range(2):
                    r = slice(s * H, (s + 1) * H)
                    m = cst[r, K_SM + SB * n:K_SM + SB * (n + 1)].bitcast(U32).rearrange("p (n h) -> p n h", h=h)\
                        .unsqueeze(1).to_broadcast([H, NC, SB // h, h])
                    last = nc.vector.copy_predicated(halves(AQ[p][r, :, r], h)[:, :, :, 1, :], m, src[r, :, 1, :, :])
                last.then_inc(S[f"ev{h}"], 1)

            def masks64(u, p):
                now(ve, u, "lv64_mm", "b2_ok")
                older(ve, u, "m64_mm")
                TT2(LT64[p][0:64, :, :], bB[0:64, :].rearrange("p (c k s) -> p c k s", c=NC, k=2)[:, :, 0, :],
                    b2n[0:64, :].unsqueeze(2).to_broadcast([64, NC, 64]), ALU.mult).then_inc(S["k64_ok"], 1)

            def inv_first(u, p):
                before(ve, u, "u1_mm")
                TT2(Tt[:, :, :], L[p][:, 0, :, :], const(K_ID64, H).unsqueeze(1).to_broadcast([P, NC, H]), ALU.add)

            def inv_t1(u, c):
                now(ve, u, "t1_mm")
                if c:
                    now(ve, c, "ssk_mm")
                before(ve, u, "m64_mm")
                TT2(Tm[:, :, :], bM[:, NC * H:2 * NC * H].rearrange("p (c s) -> p c s", c=NC),
                    const(K_ID64, H).unsqueeze(1).to_broadcast([P, NC, H]), ALU.add).then_inc(S["t1_ok"], 1)

            def inv_t(u, h):
                now(ve, u, f"t{h}_mm", f"s{h // 2}_ok" if h > 2 else "t1_ok")
                for t, bnk, half, name in ((Tm, bT, 0, "t"), (Tt, bS, 1, "s")):
                    cols = halves(t[:, :, :], h)[:, :, :, half, :]
                    last = TT2(cols, halves(bnk[:, 0:NC * H].rearrange("p (c s) -> p c s", c=NC), h)[:, :, :, half, :],
                               cols, ALU.add)
                    if name == "s" or h < 32:
                        last.then_inc(S[f"{name}{h}_ok"], 1)

            def cross(u, p):
                now(ve, u, "x_mm")
                before(ve, u, "u1_mm")
                TT2(R[:, :, :], Vn[p][:, :, :].rearrange("p (b two) v -> p b two v", two=2)[:, :, 1, :],
                    bM[:, 2 * P:4 * P].rearrange("p (b v) -> p b v", b=NB), ALU.subtract).then_inc(S["r_ok"], 1)

            def out_squares(u, p):
                now(ve, u, "osq_ok")
                TT2(osq[:, :], osq[:, :], qsq[p][:, :], ALU.add).then_inc(S["os_ok"], 1)

            def gate_out(u):
                now(ve, u, "osq_ok", "sg_ok")
                before(ve, u, "og_ok")
                STT(OGr[:, :], sg[:, :], 1.0, bS[:, :], ALU.add, ALU.mult).then_inc(S["og_raw"], 1)

            def out_norms(u):
                now(ve, u, "st_mm")
                before(ve, u, "rr_ok")
                TS(st[:, :], first_columns(bT), P * O_EPS * QK_EPS, None, ALU.add).then_inc(S["st_ok"], 1)

            def scale_out(u):
                now(ve, u, "rb_mm", "og_raw")
                TT2(OG[:, u.h, :], OGr[:, :], bT[:, :], ALU.mult).then_inc(S["og_ok"], 1)

            def step(a, b, c, d, e, p):
                if c:
                    gate_min(c)
                if d:
                    scale_out(d)
                masks(a, p, 1)
                fill = {2: ("", "k1"), 4: ("k2", "g"), 8: ("k3", "q1"), 16: ("q2", "q3"), 32: ("0", "1")}

                def between(what):
                    if what == "g":
                        gate_max(c)
                    elif what in ("0", "1"):
                        silu(c, int(what))
                    elif what:
                        conv(c, what[0], int(what[1]))

                for h in LEVELS[1:]:
                    up(a, h)
                    if c:
                        between(fill[h][0])
                    if b:
                        inv_t(b, h)
                    masks(a, p, h)
                    if h == 2:
                        silu(a, 2)
                    if c:
                        between(fill[h][1])
                up(a, 64)
                masks64(a, p)
                if c:
                    first(c)
                if b:
                    cross(b, 1 - p)
                if c:
                    for j in (1, 2, 3):
                        conv(c, "v", j)
                if c:
                    up(c, 1)
                if b:
                    out_squares(b, 1 - p)
                    gate_out(b)
                inv_first(a, p)
                if c:
                    norms(c, 1 - p)
                inv_t1(a, c)
                if b:
                    out_norms(b)
                if c:
                    masks_0(c, 1 - p)

            def expert(g, gu, e, b):
                ve.wait_ge(S["ffn_tanh"], g * ET + e + 1)
                STT(fu, ftan, 1.0, ffn_banks[e % 2][0][:, :], ALU.add, ALU.mult).then_inc(S["ffn_u"], 1)
                ve.wait_ge(S["ffn_u"], g * ET + e + 1)
                if e == 0:
                    before(ve, gu, "group_mm")
                    now(ve, b, "ksq_ok", "diag_mm", "lv1_mm", "kl2")
                STT(hid[:, e, :], fu, hidscale[:, 0:1], ffn_banks[e % 2][1][:, :], ALU.mult, ALU.mult)\
                    .then_inc(S["ffn_hid"], 1)

            def layer_stats(gu):
                ve.wait_ge(S["x_in"], gu.dma)
                before(ve, gu, "mv_ok")
                for c in range(NC):
                    last = nc.vector.bn_stats(bst[:, c, :], xt[:, c, :])
                last.then_inc(S["bn_ok"], 1)
                constant_wait(ve)
                now(ve, gu, "bn_ok")
                before(ve, gu, "xn_ok")
                for c in range(NC):
                    last = nc.vector.bn_aggr(mv[:, c, :], bst[:, c, :])
                last.then_inc(S["mv_ok"], 1)

            def layer_norm(gu):
                now(ve, gu, "rstd_ok")
                before(ve, gu, "xT_mm", "fg_mm", "beta_mm", "xh_ok")
                for c in range(NC):
                    last = TS(xn[:, c, :], xt[:, c, :], mv[:, c, 0:1], rstd[:, c:c + 1], ALU.subtract, ALU.mult)
                last.then_inc(S["xn_ok"], 1)

            def low_parts(gu):
                now(ve, gu, "xh_ok")
                TT2(xl[:, :, :], xnT[:, :, :], xh[:, :, :].bitcast(F32), ALU.subtract).then_inc(S["xl_ok"], 1)
                now(ve, gu, "ga_ok")
                TT2(fl[:, :], bG[:, :], fh[:, :].bitcast(F32), ALU.subtract).then_inc(S["fl_ok"], 1)

            def first_head(gu, u):
                gate_min(u)
                now(ve, gu, "beta_exp")
                TS(beta[:, :, :], beta[:, :, :], 1.0, None, ALU.add).then_inc(S["beta_1"], 1)
                now(ve, gu, "beta_1")
                nc.vector.reciprocal(beta[:, :, :], beta[:, :, :]).then_inc(S["beta_ok"], 1)
                now(ve, gu, "beta_ok")
                gate_max(u)
                for n in "kqv":
                    for j in (1, 2, 3):
                        conv(u, n, j)
                for i in range(2):
                    silu(u, i)
                first(u)
                norms(u, 0)
                up(u, 1)
                masks_0(u, 0)

            def group(g, more):
                gu, nu = Unit(ve, g), Unit(ve, g + 1)
                b, d = pipeline(ve, g, step, more)
                scale_out(d)
                if more:
                    layer_stats(nu)
                for e, h in enumerate(LEVELS[1:]):
                    expert(g, gu, e, b)
                    inv_t(b, h)
                    if more and h == 4:
                        layer_norm(nu)
                expert(g, gu, 5, b)
                expert(g, gu, 6, b)
                cross(b, 1)
                expert(g, gu, 7, b)
                out_squares(b, 1)
                gate_out(b)
                out_norms(b)
                if more:
                    low_parts(nu)
                scale_out(b)
                if more:
                    first_head(nu, Unit(ve, g * HEADS + HEADS, 0))
                now(ve, gu, "group_mm")
                ve.wait_ge(S["out_done"], gu.dma)
                for i in range(2):
                    last = TT2(ot[:, 2 * i:2 * i + 2, :], (bT, bS)[i][:, :].rearrange("p (c n) -> p c n", c=2),
                               xres[:, 2 * i:2 * i + 2, :], ALU.add)
                last.then_inc(S["out_ok"], 1)

            for t in (L[0], L[1], Tx):
                last = nc.vector.memset(t[:], 0.0)
            last.then_inc(S["setup_v"], 1)
            ve.wait_ge(S["wsum_ok"], 3)
            ve.wait_ge(S["wsum_mm"], 1)
            TS(wscale[:, :], bX[:, 0:3], 1.0 / (HID * EXP), 1e-8, ALU.mult, ALU.add).then_inc(S["setup_v"], 1)
            ve.wait_ge(S["setup_v"], 2)
            TS(wthr[:, 0:3], wscale[:, :], 0.5, None, ALU.mult)
            TS(wthr[:, 3:6], wscale[:, :], -0.5, None, ALU.mult).then_inc(S["setup_v"], 1)
            ve.wait_ge(S["setup_v"], 3)
            n = 3
            for i, (flat, w) in enumerate(((wup_in, wup), (wgt_in, wgt), (flat_down, wdn))):
                to = w[:, :, :].rearrange("p a b -> p (a b)")
                TS(tern[:, :], flat, wthr[:, i:i + 1], None, ALU.is_gt)
                TS(tern2[:, :], flat, wthr[:, 3 + i:4 + i], None, ALU.is_lt).then_inc(S["setup_v"], 1)
                n += 1
                ve.wait_ge(S["setup_v"], n)
                TT2(to, tern[:, :], tern2[:, :], ALU.subtract).then_inc(S["setup_v"], 1)
                n += 1
                ve.wait_ge(S["setup_v"], n)
            TS(upscale[:, :], wscale[:, 0:1], 0.5, None, ALU.mult)
            TT2(hidscale[:, :], wscale[:, 0:1], wscale[:, 1:2], ALU.mult).then_inc(S["setup_v"], 1)
            n += 1
            ve.wait_ge(S["setup_v"], n)
            STT(hidscale[:, :], hidscale[:, :], 0.5, wscale[:, 2:3], ALU.mult, ALU.mult)
            TS(wo[:, :, :], wo[:, :, :], nw[:, 0:1], 0.5, ALU.mult, ALU.mult)
            ve.wait_ge(S["wsum_ok"], 4)
            TS(smalls[:, :, C_A], smalls[:, :, C_A], -1.0, None, ALU.mult).then_inc(S["setup_ok"], 1)

            gu = Unit(ve, 0)
            layer_stats(gu)
            layer_norm(gu)
            low_parts(gu)
            first_head(gu, Unit(ve, 0, 0))
            all_groups(ve, group)

        @block.gpsimd
        def _(gp):
            GT = nc.gpsimd.tensor_tensor
            prime(gp, "POOL")

            def small_cols(u):
                constant_wait(gp)
                before(gp, u, "cv3_k", "cv3_q", "cv3_v", "g_ready")
                nc.gpsimd.tensor_copy(sm[:, :], smalls[:, u.h, :]).then_inc(S["sm_ok"], 1)

            def up(u, h):
                if h == 1:
                    now(gp, u, "g_ready", "silu_k")
                    before(gp, u, "lv128_mm", "kq4", "kl4")
                else:
                    now(gp, u, f"lv{h}_mm", f"kl{h}")
                    if h < 64:
                        before(gp, u, f"kq{4 * h}", f"kl{4 * h}")
                if h < 64:
                    g2 = halves(G[h][:, :], 1)
                    GT(G[2 * h][:, :].unsqueeze(2), g2[:, :, 0, :], g2[:, :, 1, :], ALU.mult)
                    o = halves(KL[:, :], h)[:, :, 0, :]
                    s = halves(kq[:, 0, :], h)[:, :, 0, :] if h == 1 else o
                    g = g2[:, :, 1, :].to_broadcast([P, TOK // (2 * h), h])
                else:
                    o = KL[:, :].rearrange("p (b f t) -> p b f t", b=NB, f=4)[:, :, 0, :]
                    s = o
                    g = G[64][:, :].rearrange("p (b f) -> p b f", b=NB)[:, :, 1:2].to_broadcast([P, NB, 64])
                GT(o, s, g, ALU.mult).then_inc(S[f"kl{2 * h}"], 1)

            def norms(u):
                now(gp, u, "ssk_ok")
                before(gp, u, "v_norm")
                GT(nh[:, :], ssk4[:, :], const(K_HALF, NC), ALU.pow).then_inc(S["nh_ok"], 1)

            def scaled_masks(u, i):
                now(gp, u, "b2_ok")
                before(gp, u, f"ev{LEVELS[2 * i + 1]}")
                for n in (2 * i, 2 * i + 1):
                    last = GT(mb[:, n, :, :], const(K_SM + SB * n, SB).unsqueeze(1).to_broadcast([P, NC, SB]),
                              b2n[:, :].unsqueeze(2).to_broadcast([P, NC, SB]), ALU.mult)
                last.then_inc(S[f"mb{i}"], 1)

            def scales(u):
                now(gp, u, "st_ok")
                before(gp, u, "rb_mm")
                GT(rr[:, :], st[:, :], const(K_NHALF, NC), ALU.pow).then_inc(S["rr_ok"], 1)

            def split(u, p):
                now(gp, u, "wh_hi")
                older(gp, u, "proj_v")
                GT(wlo[p][:, :], wraw[:, :], whi[p][:, :].bitcast(F32), ALU.subtract).then_inc(S["wh_lo"], 1)

            def step(a, b, c, d, e, p):
                if c:
                    small_cols(c)
                scaled_masks(a, 0)
                up(a, 2)
                scaled_masks(a, 1)
                up(a, 4)
                scaled_masks(a, 2)
                up(a, 8)
                up(a, 16)
                if e:
                    split(e, p)
                up(a, 32)
                up(a, 64)
                if c:
                    up(c, 1)
                if b:
                    scales(b)
                if c:
                    norms(c)

            def layer_rstd(g, gu):
                constant_wait(gp)
                now(gp, gu, "mv_ok")
                before(gp, gu, "xn_ok")
                nc.gpsimd.tensor_scalar(rstd[:, :], mv[:, :, 1], LN_EPS, None, ALU.add).then_inc(S["rstd_e"], 1)
                gp.wait_ge(S["rstd_e"], g + 1)
                GT(rstd[:, :], rstd[:, :], const(K_NHALF, NC), ALU.pow).then_inc(S["rstd_ok"], 1)

            def first_head(u):
                small_cols(u)
                up(u, 1)
                norms(u)

            def group(g, more):
                b, d = pipeline(gp, g, step, more)
                if more:
                    layer_rstd(g + 1, Unit(gp, g + 1))
                scales(b)
                if more:
                    first_head(Unit(gp, g * HEADS + HEADS, 0))

            gp.wait_ge(S["setup_ok"], 1)
            layer_rstd(0, Unit(gp, 0))
            for p in range(2):
                split(Unit(gp, p), p)
            first_head(Unit(gp, 0, 0))
            all_groups(gp, group)


def kernel(L0_attn_hidden_states, L0_attn_Wq, L0_attn_Wk, L0_attn_Wv, L0_attn_conv_q, L0_attn_conv_k,
           L0_attn_conv_v, L0_attn_A_log, L0_attn_Wfa, L0_attn_Wfb, L0_attn_dt_bias, L0_attn_Wb, L0_attn_Wga,
           L0_attn_Wgb, L0_attn_norm_w, L0_attn_Wo, L0_ffn_W_up, L0_ffn_W_gate, L0_ffn_W_down):
    import concourse.bacc as bacc
    from concourse.bass_utils import run_bass_kernel_spmd

    f = np.asarray
    x = f(L0_attn_hidden_states)
    groups = x.shape[0] // NB

    xg = x.reshape(groups, NC, P, HID).transpose(0, 2, 1, 3)

    def head_tiles(w):
        return f(w).reshape(-1, P, HEADS, P).transpose(2, 1, 0, 3)

    wh = np.concatenate([head_tiles(L0_attn_Wfb), head_tiles(L0_attn_Wk), head_tiles(L0_attn_Wq),
                         head_tiles(L0_attn_Wv)], axis=2).reshape(HEADS, P, WCOLS)
    wgb = head_tiles(L0_attn_Wgb).reshape(HEADS, P, P)
    small = np.zeros((P, HEADS, 16), np.float32)
    for c0, w in ((C_Q, L0_attn_conv_q), (C_K, L0_attn_conv_k), (C_V, L0_attn_conv_v)):
        small[:, :, c0:c0 + TAPS] = f(w).reshape(HEADS, P, TAPS).transpose(1, 0, 2)
    small[:, :, C_DT] = f(L0_attn_dt_bias).reshape(HEADS, P).T
    small[:, :, C_A] = np.broadcast_to(f(L0_attn_A_log).reshape(1, HEADS), (P, HEADS))

    def rows(w):
        return f(w).reshape(-1, P, w.shape[1]).transpose(1, 0, 2)

    arrays = {
        "x": xg, "wh": wh, "wgb": wgb, "small": small,
        "wfg": np.stack([rows(L0_attn_Wfa), rows(L0_attn_Wga)], axis=1),
        "wb": rows(L0_attn_Wb), "wo": rows(L0_attn_Wo), "nw": f(L0_attn_norm_w).reshape(P, 1),
        "wup": rows(f(L0_ffn_W_up).T).reshape(P, -1), "wgt": rows(f(L0_ffn_W_gate).T).reshape(P, -1), "wdn": rows(f(L0_ffn_W_down).T),
        "const": constants(),
    }
    arrays = {n: np.ascontiguousarray(a) for n, a in arrays.items()}
    nc = bacc.Bacc("TRN2", target_bir_lowering=False, num_devices=1)
    args = [nc.dram_tensor(f"{n}_dram", a.shape, F32, kind="ExternalInput").ap() for n, a in arrays.items()]
    out = nc.dram_tensor("out_dram", (groups, P, NC, HID), F32, kind="ExternalOutput").ap()
    build(nc, *args, out)
    r = run_bass_kernel_spmd(nc, [{f"{n}_dram": a for n, a in arrays.items()}], core_ids=[0])
    y = np.asarray(r.results[0]["out_dram"])
    return y.transpose(0, 2, 1, 3).reshape(x.shape)
```
